# Optimizing a Trainium2 kernel written in Bass

```python
import numpy as np
import jax
import jax.numpy as jnp

def _softmax(x, axis=-1):
    return jax.nn.softmax(x, axis=axis)

def _gelu(x):
    return jax.nn.gelu(x, approximate=True)

def _silu(x):
    return jax.nn.silu(x)

def _sigmoid(x):
    return jax.nn.sigmoid(x)

def _layernorm(x, axis=-1, eps=1e-05):
    m = jnp.mean(x, axis=axis, keepdims=True)
    v = jnp.var(x, axis=axis, keepdims=True)
    return (x - m) / jnp.sqrt(v + eps)

def _scatter_add(tgt, idx, src, axis=0):
    return tgt.at[idx].add(src)

def _segment_sum(src, seg, n):
    return jax.ops.segment_sum(src, seg, n)
kernel_name = 'mk_conv_preact_d1_conv_nhwc128_r4_3df941'

def setup_inputs(seed: int=0):
    np.random.seed(seed)
    _w = jnp.asarray

    def _rec_inputs():
        import jax
        import jax.numpy as jnp
        _gk = jax.random.key(seed)
        x = -0.0003957 + 1 * jax.random.normal(jax.random.fold_in(_gk, 1), (32, 56, 56, 32), jnp.float32)
        return x
    x = _rec_inputs()

    def _L0_conv_setup():
        import jax, jax.numpy as jnp
        import numpy as np
        M_FILTERS = 5
        key = jax.random.key(seed)
        ks = jax.random.split(key, 5)
        X = jax.random.normal(ks[0], (32, 56, 56, 32), dtype=jnp.float32)
        W = jax.random.normal(ks[1], (3, 3, 32, 32), dtype=jnp.float32) * 0.1
        beta = jax.random.normal(ks[2], (3,), dtype=jnp.float32)
        v = jax.random.normal(ks[3], (3,), dtype=jnp.float32) * 0.1
        bias = jax.random.normal(ks[4], (3,), dtype=jnp.float32) * 0.1
        return {'X': X, 'W': W, 'beta': beta, 'v': v, 'bias': bias, 'stride': 1}
    _L0_conv_all = _L0_conv_setup()
    _L0_conv_in = {k: v for k, v in _L0_conv_all.items() if k in ('W', 'beta', 'v', 'bias')}
    del _L0_conv_all
    return {'x': x, 'L0_conv_W': _L0_conv_in['W'], 'L0_conv_beta': _L0_conv_in['beta'], 'L0_conv_v': _L0_conv_in['v'], 'L0_conv_bias': _L0_conv_in['bias']}

def reference(x, L0_conv_W, L0_conv_beta, L0_conv_v, L0_conv_bias):
    import jax
    import jax.numpy as jnp

    def _L0_conv_ref(X, W, beta, v, bias, stride):
        import jax, jax.numpy as jnp
        import numpy as np
        M_FILTERS = 5
        M = M_FILTERS
        N = beta.shape[0]
        mean = jnp.mean(W)
        std = jnp.sqrt(jnp.var(W))
        us = jnp.asarray([-1.0 + i * 2.0 / (M - 1) for i in range(M)], dtype=W.dtype)
        B = jnp.sign(W[None] - mean + us[:, None, None, None, None] * std)
        Bf = B.reshape(M, -1).T
        wf = W.reshape(-1)
        alpha = jnp.linalg.solve(Bf.T @ Bf, Bf.T @ wf)
        W_eff = jnp.einsum('m,mhwio->hwio', alpha, B)
        sum_alpha = jnp.sum(alpha)

        def conv(A):
            return jax.lax.conv_general_dilated(A, W_eff, window_strides=(stride, stride), padding='SAME', dimension_numbers=('NHWC', 'HWIO', 'NHWC'))
        out = jnp.zeros(conv(jnp.zeros_like(X)).shape, dtype=X.dtype)
        for n in range(N):
            An = jnp.sign(jnp.clip(X + v[n], 0.0, 1.0) - 0.5)
            out = out + beta[n] * (conv(An) + sum_alpha * bias[n])
        return out

    def _gn(v, G=32, eps=1e-05):
        B_, H_, W_, C_ = v.shape
        g = v.reshape(B_, H_, W_, G, C_ // G)
        m = jnp.mean(g, axis=(1, 2, 4), keepdims=True)
        s = jnp.var(g, axis=(1, 2, 4), keepdims=True)
        return ((g - m) / jnp.sqrt(s + eps)).reshape(v.shape)

    def _ln_c(v, eps=1e-06):
        m = jnp.mean(v, axis=-1, keepdims=True)
        s = jnp.var(v, axis=-1, keepdims=True)
        return (v - m) / jnp.sqrt(s + eps)

    def _ln_t(v, eps=1e-05):
        m = jnp.mean(v, axis=-1, keepdims=True)
        s = jnp.var(v, axis=-1, keepdims=True)
        return (v - m) / jnp.sqrt(s + eps)

    def _to_tokens(v):
        B_, H_, W_, C_ = v.shape
        return v.reshape(B_, H_ * W_, C_)

    def _from_tokens(t, like):
        return t.reshape(like.shape)
    x = x + _L0_conv_ref(_gn(x), L0_conv_W, L0_conv_beta, L0_conv_v, L0_conv_bias, 1)
    return x

_drawn_inputs = setup_inputs


def setup_inputs(seed=0):
    import zlib

    import numpy as np

    out = dict(_drawn_inputs(seed))
    spreads = {}
    factors = {'L0_conv_bias': 34.0}
    for name, (base, spread) in spreads.items():
        noise = np.random.default_rng([zlib.crc32(name.encode()), seed]).standard_normal(out[name].shape)
        drawn = base * np.exp(spread * noise) if base else spread * noise
        out[name] = jnp.asarray(drawn.astype(out[name].dtype))
    for name, factor in factors.items():
        out[name] = (out[name] * factor).astype(out[name].dtype)
    return out
```

```python
from contextlib import ExitStack

import concourse.bass as bass
from concourse import mybir

FP32 = mybir.dt.float32
FP16 = mybir.dt.float16
ALU = mybir.AluOpType
ACT = mybir.ActivationFunctionType
AX = mybir.AxisListType

IMAGES, H, W, C = 32, 56, 56, 32
TAPS = 3
N_ACT = 3
M_FIL = 5
PAIRS = IMAGES // 2
ROWS = 2 * H
G = 4
BLOCKS = W // G
POS = BLOCKS * ROWS
HP = H + 2
BLK = 2 * HP
CHUNKS = 4
CB = [4, 4, 4, 2]
CO = [4, 4, 4, 3]
BANK = 512
UNROLL = 4
AHEAD = 3
GRID = 2.0 ** 9
LO_SCALE = 2.0 ** 10
W_SCALE = 2.0 ** 10
ROUND = 1.5 * 2.0 ** 23
GN_EPS = 1e-5


def preact_conv_kernel(nc, x, w, beta, v, bias, out):
    ctx = ExitStack()
    with ctx:
        def sb(name, shape, dt=FP32):
            return ctx.enter_context(nc.sbuf_tensor(name, shape, dt))

        def ps(name, shape):
            return ctx.enter_context(nc.psum_tensor(name, shape, FP32))

        def sem(name):
            return ctx.enter_context(nc.semaphore(name))

        x_nat = [sb(f"x_nat{i}", [ROWS, W * C]) for i in range(UNROLL)]
        y_nat = [sb(f"y_nat{i}", [ROWS, W * C]) for i in range(2)]
        x_ch = [sb(f"x_ch{i}", [128, 2, BLOCKS, H]) for i in range(2)]
        signs = [sb(f"signs{i}", [128, N_ACT, BLOCKS, 2, H], FP16) for i in range(2)]
        part1 = sb("part1", [128, POS], FP16)
        part2 = sb("part2", [128, POS], FP16)
        part3 = sb("part3", [128, POS], FP16)
        part4 = sb("part4", [128, POS], FP16)
        half_hi = sb("half_hi", [128, POS], FP16)
        s_even = [sb(f"s_even{i}", [128, 2, BLOCKS * BLK], FP16) for i in range(2)]
        s_odd = [sb(f"s_odd{i}", [128, 2, (BLOCKS + 1) * BLK], FP16) for i in range(2)]
        y_ch = [sb(f"y_ch{i}", [128, 4 * ROWS]) for i in range(2)]
        raw_stats = [sb(f"raw_stats{i}", [128, 2, 2, 6]) for i in range(2)]
        lane_stats = [sb(f"lane_stats{i}", [128, 2, 3]) for i in range(2)]
        moments = [sb(f"moments{i}", [128, 2, 2]) for i in range(2)]
        var_eps = sb("var_eps", [128, 2])
        root = sb("root", [128, 2])
        inv_root = sb("inv_root", [128, 2])
        twice_dev = sb("twice_dev", [128, 2])
        neg_thr = [sb(f"neg_thr{i}", [128, N_ACT, 2]) for i in range(2)]
        ident = sb("ident", [128, 128])
        gather = sb("gather", [128, G, G, C])
        ones = sb("ones", [128, 128])
        eps_col = sb("eps_col", [128, 1])
        params = sb("params", [128, 3, N_ACT])
        magn = sb("magn", [128, N_ACT])
        pick = sb("pick", [128, 2, N_ACT])
        order = sb("order", [128, 2, N_ACT])
        tmp = sb("tmp", [128, 8, N_ACT])
        ratio_hi = sb("ratio_hi", [128, 2])
        ratio_lo = sb("ratio_lo", [128, 2])
        w_raw = sb("w_raw", [128, TAPS, 2, C])
        filt = sb("filt", [128, M_FIL + 1, TAPS, 2, C])
        prod = sb("prod", [96, M_FIL + 1, TAPS, C])
        w_stat = sb("w_stat", [128, 16])
        w_bias = sb("w_bias", [128, M_FIL])
        gram_lane = sb("gram_lane", [96, M_FIL, M_FIL + 1])
        gram = sb("gram", [128, M_FIL, M_FIL + 1])
        outer = sb("outer", [128, M_FIL, M_FIL + 1])
        neg_row = sb("neg_row", [128, M_FIL, M_FIL + 1])
        alpha = sb("alpha", [128, M_FIL])
        inv = sb("inv", [128, 4])
        w_eff = sb("w_eff", [128, TAPS, 2, C])
        w_mm = sb("w_mm", [128, 3, TAPS, 2, C], FP16)
        y_scale = sb("y_scale", [128, 1])
        y_const = sb("y_const", [128, 1])

        x_ps = [ps(f"x_ps{i}", [128, BANK]) for i in range(2)]
        conv_ps = [ps(f"conv_ps{i}", [128, BANK]) for i in range(2)]
        y_ps = [ps(f"y_ps{i}", [128, BANK]) for i in range(2)]
        stat_ps = ps("stat_ps", [128, BANK])
        w_ps = ps("w_ps", [128, BANK])

        x_loaded = [sem(f"x_loaded{i}") for i in range(UNROLL)]
        x_transposed = sem("x_transposed")
        x_copied = [sem(f"x_copied{i}") for i in range(2)]
        lanes_ready = sem("lanes_ready")
        gathered = sem("gathered")
        moments_ready = sem("moments_ready")
        root_ready = sem("root_ready")
        thr_ready = sem("thr_ready")
        signed = sem("signed")
        s_made = sem("s_made")
        shifted = [sem(f"shifted{i}") for i in range(2)]
        conv_done = sem("conv_done")
        y_scaled = [sem(f"y_scaled{i}") for i in range(2)]
        y_transposed = sem("y_transposed")
        y_added = [sem(f"y_added{i}") for i in range(2)]
        y_stored = [sem(f"y_stored{i}") for i in range(2)]
        ident_zero, ident_ready = sem("ident_zero"), sem("ident_ready")
        gather_ready = sem("gather_ready")
        pads_ready = sem("pads_ready")
        params_loaded = sem("params_loaded")
        w_loaded = sem("w_loaded")
        consts_ready = sem("consts_ready")
        w_lane_stats = sem("w_lane_stats")
        w_summed = sem("w_summed")
        w_var_ready = sem("w_var_ready")
        w_root_ready = sem("w_root_ready")
        w_bias_ready = sem("w_bias_ready")
        w_signed = sem("w_signed")
        gram_lanes = sem("gram_lanes")
        gram_summed = sem("gram_summed")
        w_ready = sem("w_ready")
        vec = sem("vec")

        x_pairs = x.rearrange("(n a) h w c -> n (a h) (w c)", a=2)
        out_pairs = out.rearrange("(n a) h w c -> n (a h) (w c)", a=2)

        def place(j, k, depth):
            return k % depth, (UNROLL // depth) * j + k // depth

        def stages(k0):
            return dict(load=k0 + UNROLL < PAIRS and k0 >= 0, bring=k0 + AHEAD < PAIRS,
                        stats=0 <= k0 + 2 < PAIRS, weigh=0 <= k0 + 1 < PAIRS, conv=k0 >= 0)

        LOOP = 3
        FULL = dict(load=True, bring=True, stats=True, weigh=True, conv=True)

        def program(eng, step, between=None):
            for k in range(-AHEAD, 0):
                step(0, k, **stages(k))
                if k == -2 and between:
                    between()
            with eng.Fori(0, LOOP) as j:
                for k in range(UNROLL):
                    step(j, k, **FULL)
            for k in range(UNROLL):
                step(LOOP, k, **stages(UNROLL * LOOP + k))

        block = ctx.enter_context(nc.Block())

        @block.sync
        def _(sp):
            for k in range(UNROLL):
                sp.dma_start(x_nat[k][:], x_pairs[k]).then_inc(x_loaded[k], 16)

            def step(j, k, load, bring, stats, weigh, conv):
                if weigh:
                    b, uses = place(j, k + 1, 2)
                    sp.wait_ge(s_made, 2 * (4 * j + k + 2))
                    sp.dma_start(s_odd[b][0:64, :, BLK:], s_even[b][64:128, :, :]).then_inc(shifted[b], 16)
                    sp.dma_start(s_odd[b][64:128, :, 0:BLOCKS * BLK], s_even[b][0:64, :, :]).then_inc(shifted[b], 16)
                if conv:
                    b, uses = place(j, k, 2)
                    for i in range(2):
                        sp.wait_ge(y_added[i], 2 * (4 * j + k + 1))
                    if load:
                        s, _ = place(j, k, UNROLL)
                        sp.dma_start(x_nat[s][:], x_pairs[4 * j + k + UNROLL]).then_inc(x_loaded[s], 16)
                    sp.dma_start(out_pairs[4 * j + k], y_nat[b][:]).then_inc(y_stored[b], 16)

            program(sp, step)
            for b in range(2):
                sp.wait_ge(y_stored[b], 16 * PAIRS // 2)

        @block.gpsimd
        def _(pool):
            pool.memset(ident[:], 0.0).then_inc(ident_zero, 1)
            pool.wait_ge(ident_zero, 1)
            pool.affine_select(out=ident[:], in_=ident[:], compare_op=ALU.not_equal, fill=1.0, base=0,
                               pattern=[[-1, 128]], channel_multiplier=1).then_inc(ident_ready, 1)
            for i in range(2):
                for t in (s_even[i], s_odd[i]):
                    last = pool.memset(t[:], 0.0)
            last.then_inc(pads_ready, 1)

        @block.scalar
        def _(act):
            for o in range(2):
                for kw in range(TAPS):
                    g = kw + o
                    act.dma_start(w_raw[C * g:C * (g + 1), :, o, :],
                                  w[:, kw, :, :].rearrange("a i o -> i a o")).then_inc(w_loaded, 16)
            for i, p in enumerate((beta, v, bias)):
                act.dma_start(params[:, i, :], p.partition_broadcast(128)).then_inc(params_loaded, 16)

            def copy_in(j, k, c):
                q = k + AHEAD
                b, _ = place(j, q, 2)
                act.wait_ge(x_transposed, CHUNKS * (4 * j + q) + c + 1)
                n = CB[c]
                act.activation(x_ch[b][:, :, 4 * c:4 * c + n, :].rearrange("p a i h -> p i a h"),
                               x_ps[c % 2][:, 0:n * ROWS].rearrange("p (i a h) -> p i a h", a=2, h=H),
                               ACT.Copy).then_inc(x_copied[c % 2], 1)

            def sign(j, k, n, a):
                b, _ = place(j, k + 2, 2)
                act.activation(signs[b][:, n, :, a, :], x_ch[b][:, a], ACT.Sign,
                               bias=neg_thr[b][:, n, a:a + 1]).then_inc(signed, 1)

            def take_root(j, k):
                b, _ = place(j, k + 2, 2)
                act.wait_ge(moments_ready, 2 * (4 * j + k + 3))
                act.activation(root[:], moments[b][:, :, 1], ACT.Sqrt, bias=eps_col[:]).then_inc(root_ready, 1)

            def scale_out(j, k, c):
                b = c % 2
                act.wait_ge(conv_done, CHUNKS * (4 * j + k) + c + 1)
                act.wait_ge(y_transposed, CHUNKS * (4 * j + k) + max(c - 1, 0))
                n = CB[c] * ROWS
                if CO[c] > CB[c]:
                    act.activation(y_ch[b][0:C, n:n + ROWS], conv_ps[b][0:C, n:n + ROWS], ACT.Copy,
                                   scale=y_scale[0:C, :])
                act.activation(y_ch[b][:, 0:n], conv_ps[b][:, 0:n], ACT.Copy,
                               scale=y_scale[:]).then_inc(y_scaled[b], 1)

            def step(j, k, load, bring, stats, weigh, conv):
                def do_sign(n, a):
                    if stats:
                        sign(j, k, n, a)
                if conv:
                    scale_out(j, k, 0)
                if stats:
                    take_root(j, k)
                if conv:
                    scale_out(j, k, 1)
                if stats:
                    act.wait_ge(thr_ready, 3 * (4 * j + k + 3))
                    if not (isinstance(j, int) and 4 * j + k < 0):
                        act.wait_ge(s_made, 2 * (4 * j + k + 1))
                do_sign(0, 0)
                do_sign(0, 1)
                if bring:
                    copy_in(j, k, 0)
                do_sign(1, 0)
                if conv:
                    scale_out(j, k, 2)
                do_sign(1, 1)
                if bring:
                    copy_in(j, k, 1)
                do_sign(2, 0)
                do_sign(2, 1)
                if conv:
                    scale_out(j, k, 3)
                if bring:
                    copy_in(j, k, 2)
                    copy_in(j, k, 3)

            def filter_signs():
                act.wait_ge(w_var_ready, 1)
                act.activation(w_stat[:, 5:6], w_stat[:, 4:5], ACT.Sqrt).then_inc(w_root_ready, 1)
                act.wait_ge(w_bias_ready, M_FIL)
                for m in range(M_FIL):
                    act.activation(filt[:, m], w_raw[:], ACT.Sign, bias=w_bias[:, m:m + 1]).then_inc(w_signed, 1)

            act.wait_ge(consts_ready, 1)
            program(act, step, filter_signs)

        @block.vector
        def _(dve):
            done = {"n": 0, "base": 0}

            def mark(ins):
                ins.then_inc(vec, 1)
                done["n"] += 1

            def settle():
                dve.wait_ge(vec, done["base"] + done["n"])

            def link(ins):
                mark(ins)
                settle()

            tt, ts, stt = nc.vector.tensor_tensor, nc.vector.tensor_scalar, nc.vector.scalar_tensor_tensor

            nc.vector.memset(w_raw[0:C, :, 1, :], 0.0)
            nc.vector.memset(w_raw[3 * C:4 * C, :, 0, :], 0.0)
            mark(nc.vector.memset(gram_lane[:], 0.0))
            for i in range(2):
                mark(nc.vector.memset(lane_stats[i][:], 1.0))
            nc.vector.memset(ones[:], 1.0)
            nc.vector.memset(eps_col[:], GN_EPS).then_inc(consts_ready, 1)
            dve.wait_ge(ident_ready, 1)
            nc.vector.tensor_copy(gather[:], ident[:].rearrange("p (g c) -> p g c", g=G).unsqueeze(2)
                                  .broadcast_to([128, G, G, C])).then_inc(gather_ready, 1)

            dve.wait_ge(params_loaded, 48)
            b_, v_ = params[:, 0, :], params[:, 1, :]
            link(stt(magn[:], b_, -1.0, b_, ALU.mult, ALU.max))
            link(tt(tmp[:, 0, 0:1], magn[:, 1:2], magn[:, 2:3], ALU.max))
            link(tt(pick[:, 0, 0:1], magn[:, 0:1], tmp[:, 0, 0:1], ALU.is_ge))
            link(ts(pick[:, 1, 0:1], pick[:, 0, 0:1], -1.0, 1.0, ALU.mult, ALU.add))
            link(tt(tmp[:, 0, 1:2], magn[:, 1:2], magn[:, 2:3], ALU.is_ge))
            link(tt(pick[:, 0, 1:2], tmp[:, 0, 1:2], pick[:, 1, 0:1], ALU.mult))
            link(tt(pick[:, 0, 2:3], pick[:, 1, 0:1], pick[:, 0, 1:2], ALU.subtract))
            link(ts(pick[:, 1, 1:3], pick[:, 0, 1:3], -1.0, 1.0, ALU.mult, ALU.add))
            link(nc.vector.tensor_copy(tmp[:, 1, :], b_))
            link(ts(tmp[:, 2, :], v_, 0.5, 0.5, ALU.subtract, ALU.mult))
            for i in range(2):
                src = tmp[:, 1 + i, :]
                link(tt(tmp[:, 3, :], src, pick[:, 0, :], ALU.mult))
                link(nc.vector.reduce_sum(order[:, i, 0:1], tmp[:, 3, :], axis=AX.X))
                link(tt(tmp[:, 4, 1:3], src[:, 1:3], pick[:, 1, 1:3], ALU.mult))
                link(stt(order[:, i, 1:3], pick[:, 0, 1:3], src[:, 0:1], tmp[:, 4, 1:3], ALU.mult, ALU.add))
            link(ts(tmp[:, 5, 0:1], order[:, 0, 0:1], 0.0, None, ALU.is_equal))
            link(tt(tmp[:, 5, 1:2], tmp[:, 5, 0:1], order[:, 0, 0:1], ALU.add))
            link(nc.vector.reciprocal(tmp[:, 5, 2:3], tmp[:, 5, 1:2]))
            link(ts(tmp[:, 6, 0:2], order[:, 0, 1:3], tmp[:, 5, 2:3], None, ALU.mult))
            link(ts(tmp[:, 7, 0:2], tmp[:, 6, 0:2], GRID, ROUND, ALU.mult, ALU.add))
            link(ts(ratio_hi[:], tmp[:, 7, 0:2], ROUND, 1.0 / GRID, ALU.subtract, ALU.mult))
            link(tt(tmp[:, 3, 0:2], tmp[:, 6, 0:2], ratio_hi[:], ALU.subtract))
            link(ts(ratio_lo[:], tmp[:, 3, 0:2], LO_SCALE, None, ALU.mult))

            def pair_lanes(j, k):
                q = 4 * j + k + 2
                b, _ = place(j, k + 2, 2)
                for i in range(2):
                    dve.wait_ge(x_copied[i], 2 * (q + 1))
                for a in range(2):
                    for i in range(2):
                        mark(nc.vector.bn_stats(raw_stats[b][:, a, i, :],
                                                x_ch[b][:, a, 7 * i:7 * i + 7, :].rearrange("p i h -> p (i h)")))

            def pair_lanes_end(j, k):
                b, _ = place(j, k + 2, 2)
                for a in range(2):
                    nc.vector.bn_aggr(lane_stats[b][:, a, 1:3],
                                      raw_stats[b][:, a].rearrange("p i s -> p (i s)")).then_inc(lanes_ready, 1)

            def pair_moments(j, k):
                q = 4 * j + k + 2
                b, _ = place(j, k + 2, 2)
                st = stat_ps[:, 0:G * 6].rearrange("p (g a s) -> p g a s", g=G, a=2)
                for a in range(2):
                    nc.vector.bn_aggr(moments[b][:, a, :], st[:, :, a, :]).then_inc(moments_ready, 1)

            def pair_var(j, k):
                q = 4 * j + k + 2
                b, _ = place(j, k + 2, 2)
                dve.wait_ge(moments_ready, 2 * (q + 1))
                mark(ts(var_eps[:], moments[b][:, :, 1], GN_EPS, None, ALU.add))

            def pair_recip(j, k):
                dve.wait_ge(root_ready, 4 * j + k + 3)
                mark(nc.vector.reciprocal(inv_root[:], root[:]))

            def pair_quot(j, k):
                settle()
                mark(tt(twice_dev[:], var_eps[:], inv_root[:], ALU.mult))

            def pair_dev(j, k):
                settle()
                mark(tt(twice_dev[:], twice_dev[:], root[:], ALU.add))

            def pair_thr(j, k):
                b, _ = place(j, k + 2, 2)
                settle()
                for n in range(N_ACT):
                    stt(neg_thr[b][:, n, :], twice_dev[:], order[:, 1, n:n + 1], moments[b][:, :, 0],
                        ALU.mult, ALU.subtract).then_inc(thr_ready, 1)

            def flat(b, n):
                return signs[b][:, n].rearrange("p i a h -> p (i a h)")

            def rows_of(b, s):
                return s_even[b][:, s, :].rearrange("p (r h) -> p r h", h=HP)[:, :, 1:1 + H]

            def as_rows(t):
                return t.rearrange("p (r h) -> p r h", h=H)

            def add_x(j, k, c):
                b, uses = place(j, k, 2)
                s, _ = place(j, k, UNROLL)
                dve.wait_ge(y_transposed, CHUNKS * (4 * j + k) + c + 1)
                lo, hi = max(16 * c - 1, 0), min(16 * c + 15, W)
                off = C if c == 0 else 0
                stt(y_nat[b][:, C * lo:C * hi], y_ps[c % 2][0:ROWS, off:off + C * (hi - lo)],
                    y_const[0:ROWS, :], x_nat[s][:, C * lo:C * hi],
                    ALU.add, ALU.add).then_inc(y_added[c % 2], 1)

            def step(j, k, load, bring, stats, weigh, conv):
                r = 4 * j + k + 1
                b, _ = place(j, k + 1, 2)
                if stats:
                    pair_lanes(j, k)
                if weigh:
                    dve.wait_ge(signed, 6 * (r + 1))
                    mark(ts(part1[:], flat(b, 1), ratio_hi[:, 0:1], None, ALU.mult))
                    mark(ts(part2[:], flat(b, 2), ratio_hi[:, 1:2], None, ALU.mult))
                settle()
                if weigh:
                    mark(ts(part3[:], flat(b, 1), ratio_lo[:, 0:1], None, ALU.mult))
                if stats:
                    pair_lanes_end(j, k)
                if weigh:
                    mark(ts(part4[:], flat(b, 2), ratio_lo[:, 1:2], None, ALU.mult))
                if stats:
                    dve.wait_ge(gathered, r + 2)
                if weigh:
                    mark(tt(half_hi[:], part1[:], part2[:], ALU.add))
                if stats:
                    pair_moments(j, k)
                    pair_var(j, k)
                if weigh:
                    settle()
                    if conv:
                        dve.wait_ge(conv_done, CHUNKS * (r - 1))
                    elif k == -1:
                        dve.wait_ge(pads_ready, 1)
                    tt(rows_of(b, 0), as_rows(half_hi[:]), rows_of_sign(b), ALU.add).then_inc(s_made, 1)
                if conv:
                    dve.wait_ge(y_stored[place(j, k, 2)[0]], 16 * place(j, k, 2)[1])
                    add_x(j, k, 0)
                if stats:
                    pair_recip(j, k)
                    pair_quot(j, k)
                    pair_dev(j, k)
                    pair_thr(j, k)
                if weigh:
                    tt(rows_of(b, 1), as_rows(part3[:]), as_rows(part4[:]), ALU.add).then_inc(s_made, 1)
                if conv:
                    for c in range(1, CHUNKS):
                        add_x(j, k, c)

            def rows_of_sign(b):
                return signs[b][:, 0].rearrange("p i a h -> p (i a) h")

            def make_filter():
                lanes = w_raw[0:96, :, 0, :]
                dve.wait_ge(w_loaded, 96)
                link(nc.vector.bn_stats(w_stat[0:96, 6:12], lanes))
                link(nc.vector.bn_aggr(w_stat[0:96, 0:2], w_stat[0:96, 6:12]))
                link(tt(w_stat[0:96, 2:3], w_stat[0:96, 0:1], w_stat[0:96, 0:1], ALU.mult))
                link(tt(w_stat[0:96, 1:2], w_stat[0:96, 1:2], w_stat[0:96, 2:3], ALU.add))
                nc.vector.tensor_copy(filt[:, M_FIL], w_raw[:]).then_inc(w_lane_stats, 1)
                dve.wait_ge(w_summed, 1)
                link(ts(w_stat[:, 12:14], w_ps[:, 0:2], 1.0 / 96, None, ALU.mult))
                link(tt(w_stat[:, 3:4], w_stat[:, 12:13], w_stat[:, 12:13], ALU.mult))
                tt(w_stat[:, 4:5], w_stat[:, 13:14], w_stat[:, 3:4], ALU.subtract).then_inc(w_var_ready, 1)
                dve.wait_ge(w_root_ready, 1)
                dve.wait_ge(w_var_ready, 1)
                link(nc.vector.reciprocal(w_stat[:, 14:15], w_stat[:, 5:6]))
                link(tt(w_stat[:, 14:15], w_stat[:, 14:15], w_stat[:, 4:5], ALU.mult))
                link(tt(w_stat[:, 15:16], w_stat[:, 14:15], w_stat[:, 5:6], ALU.add))
                for m in range(M_FIL):
                    u = -1.0 + m * 2.0 / (M_FIL - 1)
                    stt(w_bias[:, m:m + 1], w_stat[:, 15:16], 0.5 * u, w_stat[:, 12:13],
                        ALU.mult, ALU.subtract).then_inc(w_bias_ready, 1)
                for m in range(M_FIL):
                    n = M_FIL + 1 - m
                    dve.wait_ge(w_signed, M_FIL)
                    me = filt[0:96, m, :, 0, :]
                    for t in range(n):
                        mark(tt(prod[:, m + t], filt[0:96, m + t, :, 0, :], me, ALU.mult))
                    settle()
                    link(nc.vector.reduce_sum(gram_lane[:, m, m:], prod[:, m:].rearrange("p m a c -> p m (a c)"),
                                              axis=AX.X))
                nc.vector.tensor_copy(inv[0:96, 3:4], gram_lane[:, 0, 0:1]).then_inc(gram_lanes, 1)
                dve.wait_ge(gram_summed, 1)
                link(nc.vector.tensor_copy(gram[:], w_ps[:, 0:30].rearrange("p (m n) -> p m n", m=M_FIL)))
                for m in range(M_FIL):
                    link(nc.vector.reciprocal(inv[:, 0:1], gram[:, m, m:m + 1]))
                    link(ts(neg_row[:, m, m:], gram[:, m, m:], inv[:, 0:1], -1.0, ALU.mult, ALU.mult))
                    r = M_FIL - 1 - m
                    if r:
                        col = gram[:, m, m + 1:M_FIL].unsqueeze(2).broadcast_to([128, r, r + 1])
                        row = neg_row[:, m, m + 1:].unsqueeze(1).broadcast_to([128, r, r + 1])
                        link(tt(outer[:, m + 1:, m + 1:], col, row, ALU.mult))
                        link(tt(gram[:, m + 1:, m + 1:], gram[:, m + 1:, m + 1:], outer[:, m + 1:, m + 1:], ALU.add))
                link(ts(alpha[:], neg_row[:, :, M_FIL], -1.0, None, ALU.mult))
                for m in range(M_FIL - 1, 0, -1):
                    link(stt(alpha[:, 0:m], neg_row[:, 0:m, m], alpha[:, m:m + 1], alpha[:, 0:m], ALU.mult, ALU.add))
                flat_w = w_eff[:].rearrange("p a o c -> p (a o c)")
                fl = [filt[:, m].rearrange("p a o c -> p (a o c)") for m in range(M_FIL)]
                link(ts(flat_w, fl[0], alpha[:, 0:1], None, ALU.mult))
                for m in range(1, M_FIL):
                    link(stt(flat_w, fl[m], alpha[:, m:m + 1], flat_w, ALU.mult, ALU.add))
                link(stt(w_stat[:, 6:11], alpha[:], -1.0, alpha[:], ALU.mult, ALU.max))
                link(nc.vector.reduce_sum(inv[:, 1:2], w_stat[:, 6:11], axis=AX.X))
                link(nc.vector.reciprocal(inv[:, 2:3], inv[:, 1:2]))
                link(ts(flat_w, flat_w, inv[:, 2:3], W_SCALE, ALU.mult, ALU.mult))
                wm = [w_mm[:, i].rearrange("p a o c -> p (a o c)") for i in range(3)]
                link(nc.vector.tensor_copy(wm[0], flat_w))
                mark(tt(wm[1], flat_w, wm[0], ALU.subtract))
                link(ts(wm[2], wm[0], 1.0 / LO_SCALE, None, ALU.mult))
                for i in range(3):
                    mark(nc.vector.memset(w_mm[0:C, i, :, 1, :], 0.0))
                    mark(nc.vector.memset(w_mm[3 * C:4 * C, i, :, 0, :], 0.0))
                mark(ts(y_scale[:], inv[:, 1:2], order[:, 0, 0:1], 1.0 / W_SCALE, ALU.mult, ALU.mult))
                link(nc.vector.reduce_sum(w_stat[:, 0:1], alpha[:], axis=AX.X))
                link(tt(tmp[:, 0, :], params[:, 0, :], params[:, 2, :], ALU.mult))
                link(nc.vector.reduce_sum(w_stat[:, 1:2], tmp[:, 0, :], axis=AX.X))
                tt(y_const[:], w_stat[:, 0:1], w_stat[:, 1:2], ALU.mult).then_inc(w_ready, 1)
                dve.wait_ge(w_ready, 1)

            for k in range(-AHEAD, 0):
                step(0, k, **stages(k))
                if k == -2:
                    make_filter()
            start = done["n"]
            with dve.Fori(0, LOOP) as j:
                per_iteration = 0
                per_iteration = UNROLL * MARKS_PER_STEP
                done["base"] = per_iteration * j
                for k in range(UNROLL):
                    step(j, k, **FULL)
                assert done["n"] - start == per_iteration, done["n"] - start
            done["base"] = 0
            done["n"] = start + per_iteration * LOOP
            for k in range(UNROLL):
                step(LOOP, k, **stages(UNROLL * LOOP + k))

        @block.tensor
        def _(pe):
            def bring_in(j, k, c):
                q = k + AHEAD
                s, uses = place(j, q, UNROLL)
                if c == 0:
                    pe.wait_ge(x_loaded[s], 16 * (uses + 1))
                if not (isinstance(j, int) and 4 * j + q == 0 and c < 2):
                    pe.wait_ge(x_copied[c % 2], 2 * (4 * j + q) + c // 2)
                for i in range(CB[c]):
                    blk = 4 * c + i
                    last = nc.tensor.transpose(x_ps[c % 2][:, i * ROWS:(i + 1) * ROWS],
                                               x_nat[s][:, 128 * blk:128 * (blk + 1)], ident[0:ROWS, 0:ROWS])
                last.then_inc(x_transposed, 1)

            def gather_lanes(j, k):
                q = 4 * j + k + 2
                b, _ = place(j, k + 2, 2)
                pe.wait_ge(lanes_ready, 2 * (q + 1))
                if not (isinstance(j, int) and q == 0):
                    pe.wait_ge(moments_ready, 2 * q)
                for g in range(G):
                    last = nc.tensor.matmul(stat_ps[:, 6 * g:6 * g + 6],
                                            gather[:, g].rearrange("p r c -> p (r c)"),
                                            lane_stats[b][:].rearrange("p a s -> p (a s)"), start=True, stop=True)
                last.then_inc(gathered, 1)

            PRODUCTS = [(0, 0), (0, 1), (1, 2)]

            def convolve(j, k, c):
                b, uses = place(j, k, 2)
                bank = c % 2
                if c == 0:
                    pe.wait_ge(s_made, 2 * (4 * j + k + 1))
                    pe.wait_ge(shifted[b], 32 * (uses + 1))
                pe.wait_ge(y_scaled[bank], 2 * (4 * j + k) + c // 2)
                even = s_even[b][:].rearrange("p s (r h) -> p s r h", h=HP)
                odd = s_odd[b][:].rearrange("p s (r h) -> p s r h", h=HP)
                for n, (part, kind) in enumerate(PRODUCTS):
                    for t in range(TAPS):
                        first, end = n == 0 and t == 0, n == 2 and t == TAPS - 1
                        wt = w_mm[:, kind, t].rearrange("p o c -> p (o c)")
                        r0 = 2 * 4 * c
                        nc.tensor.matmul(conv_ps[bank][0:64, 0:CO[c] * ROWS], wt,
                                         odd[:, part, r0:r0 + 2 * CO[c], t:t + H], start=first, stop=end)
                        last = nc.tensor.matmul(conv_ps[bank][64:128, 0:CB[c] * ROWS], wt,
                                                even[:, part, r0:r0 + 2 * CB[c], t:t + H], start=first, stop=end)
                last.then_inc(conv_done, 1)

            def bring_out(j, k, c):
                bank = c % 2
                pe.wait_ge(y_scaled[bank], 2 * (4 * j + k) + c // 2 + 1)
                pe.wait_ge(y_added[bank], 2 * (4 * j + k) + c // 2)
                for i in range(CO[c]):
                    p = 128 if i < CB[c] else C
                    last = nc.tensor.transpose(y_ps[bank][0:ROWS, 128 * i:128 * i + p],
                                               y_ch[bank][0:p, i * ROWS:(i + 1) * ROWS], ident[0:p, 0:p])
                last.then_inc(y_transposed, 1)

            def step(j, k, load, bring, stats, weigh, conv):
                if conv:
                    convolve(j, k, 0)
                if stats:
                    gather_lanes(j, k)
                if conv:
                    convolve(j, k, 1)
                if bring:
                    bring_in(j, k, 0)
                if conv:
                    bring_out(j, k, 0)
                    convolve(j, k, 2)
                if bring:
                    bring_in(j, k, 1)
                if conv:
                    bring_out(j, k, 1)
                    convolve(j, k, 3)
                if bring:
                    bring_in(j, k, 2)
                if conv:
                    bring_out(j, k, 2)
                if bring:
                    bring_in(j, k, 3)
                if conv:
                    bring_out(j, k, 3)

            def filter_sums():
                pe.wait_ge(w_lane_stats, 1)
                nc.tensor.matmul(w_ps[:, 0:2], ones[0:96, :], w_stat[0:96, 0:2], start=True, stop=True)\
                    .then_inc(w_summed, 1)
                pe.wait_ge(gram_lanes, 1)
                nc.tensor.matmul(w_ps[:, 0:30], ones[0:96, :], gram_lane[:].rearrange("p m n -> p (m n)"),
                                 start=True, stop=True).then_inc(gram_summed, 1)

            pe.wait_ge(ident_ready, 1)
            pe.wait_ge(gather_ready, 1)
            for k in range(-AHEAD, 0):
                step(0, k, **stages(k))
                if k == -2:
                    filter_sums()
            pe.wait_ge(w_ready, 1)
            with pe.Fori(0, LOOP) as j:
                for k in range(UNROLL):
                    step(j, k, **FULL)
            for k in range(UNROLL):
                step(LOOP, k, **stages(UNROLL * LOOP + k))


MARKS_PER_STEP = 13


_INS = ["x", "L0_conv_W", "L0_conv_beta", "L0_conv_v", "L0_conv_bias"]


def kernel(**inputs):
    import numpy as np
    import concourse.bacc as bacc
    from concourse.bass_utils import run_bass_kernel_spmd

    nc = bacc.Bacc("TRN2", target_bir_lowering=False, num_devices=1)
    arrays, args = {}, []
    for name in _INS:
        a = np.ascontiguousarray(inputs[name])
        arrays[f"in_{name}"] = a
        args.append(nc.dram_tensor(f"in_{name}", a.shape, mybir.dt.from_np(a.dtype), kind="ExternalInput").ap())
    out = nc.dram_tensor("out_0", inputs["x"].shape, FP32, kind="ExternalOutput").ap()
    preact_conv_kernel(nc, *args, out)
    r = run_bass_kernel_spmd(nc, [arrays], core_ids=[0])
    return r.results[0]["out_0"]
```

```python
from contextlib import ExitStack

import concourse.bass as bass
from concourse import mybir

FP32 = mybir.dt.float32
FP16 = mybir.dt.float16
ALU = mybir.AluOpType
ACT = mybir.ActivationFunctionType
AX = mybir.AxisListType

IMAGES, H, W, C = 32, 56, 56, 32
TAPS = 3
N_ACT = 3
M_FIL = 5
PAIRS = IMAGES // 2
ROWS = 2 * H
G = 4
BLOCKS = W // G
POS = BLOCKS * ROWS
HP = H + 2
BLK = 2 * HP
CHUNKS = 4
CB = [4, 4, 4, 2]
CO = [4, 4, 4, 3]
BANK = 512
UNROLL = 4
AHEAD = 3
GRID = 2.0 ** 9
LO_SCALE = 2.0 ** 10
W_SCALE = 2.0 ** 10
ROUND = 1.5 * 2.0 ** 23
GN_EPS = 1e-5


def preact_conv_kernel(nc, x, w, beta, v, bias, out):
    ctx = ExitStack()
    with ctx:
        def sb(name, shape, dt=FP32):
            return ctx.enter_context(nc.sbuf_tensor(name, shape, dt))

        def ps(name, shape):
            return ctx.enter_context(nc.psum_tensor(name, shape, FP32))

        def sem(name):
            return ctx.enter_context(nc.semaphore(name))

        x_nat = [sb(f"x_nat{i}", [ROWS, W * C]) for i in range(UNROLL)]
        y_nat = [sb(f"y_nat{i}", [ROWS, W * C]) for i in range(2)]
        x_ch = [sb(f"x_ch{i}", [128, 2, BLOCKS, H]) for i in range(2)]
        signs = [sb(f"signs{i}", [128, N_ACT, BLOCKS, 2, H], FP16) for i in range(2)]
        part1 = sb("part1", [128, POS], FP16)
        part2 = sb("part2", [128, POS], FP16)
        part3 = sb("part3", [128, POS], FP16)
        part4 = sb("part4", [128, POS], FP16)
        half_hi = sb("half_hi", [128, POS], FP16)
        s_even = [sb(f"s_even{i}", [128, 2, BLOCKS * BLK], FP16) for i in range(2)]
        s_odd = [sb(f"s_odd{i}", [128, 2, (BLOCKS + 1) * BLK], FP16) for i in range(2)]
        y_ch = [sb(f"y_ch{i}", [128, 4 * ROWS]) for i in range(2)]
        raw_stats = [sb(f"raw_stats{i}", [128, 2, 2, 6]) for i in range(2)]
        lane_stats = [sb(f"lane_stats{i}", [128, 2, 3]) for i in range(2)]
        spread_stats = [sb(f"spread_stats{i}", [128, G, 6]) for i in range(2)]
        moments = [sb(f"moments{i}", [128, 2, 2]) for i in range(2)]
        var_eps = sb("var_eps", [128, 2])
        root = sb("root", [128, 2])
        inv_root = sb("inv_root", [128, 2])
        twice_dev = sb("twice_dev", [128, 2])
        neg_thr = [sb(f"neg_thr{i}", [128, N_ACT, 2]) for i in range(2)]
        ident = sb("ident", [128, 128])
        own_group = sb("own_group", [128, G])
        same_ch = sb("same_ch", [128, G, C])
        same_ch_row = sb("same_ch_row", [128, C])
        wait_carrier = sb("wait_carrier", [128, 2, 2])
        opening = sb("opening", [128, 8])
        ones = sb("ones", [128, 128])
        eps_col = sb("eps_col", [128, 1])
        params = sb("params", [128, 3, N_ACT])
        magn = sb("magn", [128, N_ACT])
        pick = sb("pick", [128, 2, N_ACT])
        order = sb("order", [128, 2, N_ACT])
        tmp = sb("tmp", [128, 9, N_ACT])
        ratio_hi = sb("ratio_hi", [128, 2])
        ratio_lo = sb("ratio_lo", [128, 2])
        w_raw = sb("w_raw", [128, TAPS, 2, C])
        filt = sb("filt", [128, M_FIL + 1, TAPS, 2, C])
        prod = sb("prod", [96, M_FIL + 1, TAPS, C])
        w_stat = sb("w_stat", [128, 16])
        w_bias = sb("w_bias", [128, M_FIL])
        gram_lane = sb("gram_lane", [96, M_FIL, M_FIL + 1])
        gram = sb("gram", [128, M_FIL, M_FIL + 1])
        outer = sb("outer", [128, M_FIL, M_FIL + 1])
        neg_row = sb("neg_row", [128, M_FIL, M_FIL + 1])
        alpha = sb("alpha", [128, M_FIL])
        inv = sb("inv", [128, 4])
        w_eff = sb("w_eff", [128, TAPS, 2, C])
        w_mm = sb("w_mm", [128, 3, TAPS, 2, C], FP16)
        y_scale = sb("y_scale", [128, 1])
        y_const = sb("y_const", [128, 1])

        x_ps = [ps(f"x_ps{i}", [128, BANK]) for i in range(2)]
        conv_ps = [ps(f"conv_ps{i}", [128, BANK]) for i in range(2)]
        y_ps = [ps(f"y_ps{i}", [128, BANK]) for i in range(2)]
        stat_ps = ps("stat_ps", [128, BANK])
        w_ps = ps("w_ps", [128, BANK])

        x_loaded = [sem(f"x_loaded{i}") for i in range(UNROLL)]
        x_transposed = sem("x_transposed")
        x_copied = [sem(f"x_copied{i}") for i in range(2)]
        lanes_ready = sem("lanes_ready")
        gathered = sem("gathered")
        moments_ready = sem("moments_ready")
        root_ready = sem("root_ready")
        thr_ready = sem("thr_ready")
        signed = sem("signed")
        hi_made, lo_made = sem("hi_made"), sem("lo_made")
        shifted_hi = [sem(f"shifted_hi{i}") for i in range(2)]
        shifted_lo = [sem(f"shifted_lo{i}") for i in range(2)]
        conv_done = sem("conv_done")
        y_scaled = [sem(f"y_scaled{i}") for i in range(2)]
        y_transposed = sem("y_transposed")
        y_added = [sem(f"y_added{i}") for i in range(2)]
        y_stored = [sem(f"y_stored{i}") for i in range(2)]
        ident_zero, ident_ready = sem("ident_zero"), sem("ident_ready")
        same_ch_ready = sem("same_ch_ready")
        pads_ready = sem("pads_ready")
        ratios_ready = sem("ratios_ready")
        params_loaded = sem("params_loaded")
        w_loaded = sem("w_loaded")
        consts_ready = sem("consts_ready")
        w_lane_stats = sem("w_lane_stats")
        w_summed = sem("w_summed")
        w_var_ready = sem("w_var_ready")
        w_root_ready = sem("w_root_ready")
        w_bias_ready = sem("w_bias_ready")
        w_signed = sem("w_signed")
        gram_lanes = sem("gram_lanes")
        gram_summed = sem("gram_summed")
        w_ready = sem("w_ready")
        vec = sem("vec")
        lo_parts = sem("lo_parts")

        x_pairs = x.rearrange("(n a) h w c -> n (a h) (w c)", a=2)
        out_pairs = out.rearrange("(n a) h w c -> n (a h) (w c)", a=2)

        OPEN = 1

        def place(j, k, depth):
            return k % depth, (UNROLL // depth) * j + k // depth

        def stages(k0):
            return dict(load=k0 + UNROLL < PAIRS and k0 >= 0, bring=k0 + AHEAD < PAIRS,
                        stats=0 <= k0 + 2 < PAIRS, weigh=0 <= k0 + 1 < PAIRS, conv=k0 >= 0)

        HALF = C * 31
        LOOP = 3
        FULL = dict(load=True, bring=True, stats=True, weigh=True, conv=True)

        def main_steps(eng, step):
            with eng.Fori(0, LOOP) as j:
                for k in range(UNROLL):
                    step(j, k, **FULL)
            for k in range(UNROLL):
                step(LOOP, k, **stages(UNROLL * LOOP + k))

        def program(eng, step):
            for k in range(-AHEAD, 0):
                step(0, k, **stages(k))
            main_steps(eng, step)

        def load_filter(eng, o):
            eng.dma_start(w_raw[C * o:C * (o + TAPS), :, o, :], w.rearrange("a k i o -> (k i) a o"))\
                .then_inc(w_loaded, 16)

        block = ctx.enter_context(nc.Block())

        @block.sync
        def _(sp):
            load_filter(sp, 0)
            for k in range(UNROLL):
                sp.dma_start(x_nat[k][:], x_pairs[k]).then_inc(x_loaded[k], 16)

            def step(j, k, load, bring, stats, weigh, conv):
                if weigh:
                    b, uses = place(j, k + 1, 2)
                    for part, made, shifted in ((0, hi_made, shifted_hi), (1, lo_made, shifted_lo)):
                        sp.wait_ge(made, 4 * j + k + 2)
                        sp.dma_start(s_odd[b][0:64, part, BLK:], s_even[b][64:128, part, :])\
                            .then_inc(shifted[b], 16)
                        sp.dma_start(s_odd[b][64:128, part, 0:BLOCKS * BLK], s_even[b][0:64, part, :])\
                            .then_inc(shifted[b], 16)
                if conv:
                    b, uses = place(j, k, 2)
                    sp.wait_ge(y_added[1], OPEN + 2 * (4 * j + k) + 1)
                    sp.dma_start(out_pairs[4 * j + k][:, 0:HALF], y_nat[b][:, 0:HALF]).then_inc(y_stored[b], 16)
                    sp.wait_ge(y_added[1], OPEN + 2 * (4 * j + k + 1))
                    if load:
                        s, _ = place(j, k, UNROLL)
                        sp.dma_start(x_nat[s][:], x_pairs[4 * j + k + UNROLL]).then_inc(x_loaded[s], 16)
                    sp.dma_start(out_pairs[4 * j + k][:, HALF:], y_nat[b][:, HALF:]).then_inc(y_stored[b], 16)

            program(sp, step)
            for b in range(2):
                sp.wait_ge(y_stored[b], 16 * (OPEN + PAIRS))

        @block.gpsimd
        def _(pool):
            pool.memset(ident[:], 0.0).then_inc(ident_zero, 1)
            pool.wait_ge(ident_zero, 1)
            pool.affine_select(out=ident[:], in_=ident[:], compare_op=ALU.not_equal, fill=1.0, base=0,
                               pattern=[[-1, 128]], channel_multiplier=1).then_inc(ident_ready, 1)
            for i, (s, n) in enumerate([(conv_done, 1), (y_transposed, 1), (y_scaled[0], 1), (y_scaled[1], 1),
                                        (y_added[0], 1), (y_added[1], 1), (y_stored[0], 16), (y_stored[1], 16)]):
                pool.memset(opening[:, i:i + 1], 0.0).then_inc(s, n)
            for t in (s_odd[0], s_odd[1], s_even[0], s_even[1]):
                pool.memset(t[:], 0.0).then_inc(pads_ready, 1)
            pool.wait_ge(ratios_ready, 1)

            def step(j, k, load, bring, stats, weigh, conv):
                if not weigh:
                    return
                r = 4 * j + k + 1
                b, _ = place(j, k + 1, 2)
                if conv:
                    pool.wait_ge(lo_made, r)
                    pool.wait_ge(conv_done, OPEN + CHUNKS * (r - 1))
                else:
                    pool.wait_ge(pads_ready, 4)
                for n, part in ((1, part3), (2, part4)):
                    pool.wait_ge(signed, 6 * r + 2 * n)
                    pool.tensor_tensor(wait_carrier[:, n - 1, :], ratio_lo[:], ratio_lo[:], ALU.add)
                    pool.tensor_scalar(part[:], signs[b][:, n].rearrange("p i a h -> p (i a h)"),
                                       ratio_lo[:, n - 1:n], 1.0, ALU.mult, ALU.mult).then_inc(lo_parts, 1)
                pool.wait_ge(lo_parts, 2 * (r + 1))
                pool.tensor_tensor(s_even[b][:, 1, :].rearrange("p (r h) -> p r h", h=HP)[:, :, 1:1 + H],
                                   part3[:].rearrange("p (r h) -> p r h", h=H),
                                   part4[:].rearrange("p (r h) -> p r h", h=H), ALU.add).then_inc(lo_made, 1)

            program(pool, step)

        @block.scalar
        def _(act):
            load_filter(act, 1)
            for i, p in enumerate((beta, v, bias)):
                act.dma_start(params[:, i, :], p.partition_broadcast(128)).then_inc(params_loaded, 16)

            def copy_in(j, k, c):
                q = k + AHEAD
                b, _ = place(j, q, 2)
                if c == 0 and not (isinstance(j, int) and 4 * j + q < 2):
                    act.wait_ge(signed, 6 * (4 * j + q - 1))
                act.wait_ge(x_transposed, CHUNKS * (4 * j + q) + c + 1)
                n = CB[c]
                act.activation(x_ch[b][:, :, 4 * c:4 * c + n, :].rearrange("p a i h -> p i a h"),
                               x_ps[c % 2][:, 0:n * ROWS].rearrange("p (i a h) -> p i a h", a=2, h=H),
                               ACT.Copy).then_inc(x_copied[c % 2], 1)

            def sign(j, k, n, a):
                b, _ = place(j, k, 2)
                act.activation(signs[b][:, n, :, a, :], x_ch[b][:, a], ACT.Sign,
                               bias=neg_thr[b][:, n, a:a + 1]).then_inc(signed, 1)

            def take_root(j, k):
                b, _ = place(j, k + 2, 2)
                act.wait_ge(moments_ready, 2 * (4 * j + k + 3))
                act.activation(root[:], moments[b][:, :, 1], ACT.Sqrt, bias=eps_col[:]).then_inc(root_ready, 1)

            def scale_out(j, k, c):
                b = c % 2
                act.wait_ge(conv_done, OPEN + CHUNKS * (4 * j + k) + c + 1)
                act.wait_ge(y_transposed, OPEN + CHUNKS * (4 * j + k) + c - 1 if c else
                            OPEN + CHUNKS * (4 * j + k))
                n = CB[c] * ROWS
                if CO[c] > CB[c]:
                    act.activation(y_ch[b][0:C, n:n + ROWS], conv_ps[b][0:C, n:n + ROWS], ACT.Copy,
                                   scale=y_scale[0:C, :])
                act.activation(y_ch[b][:, 0:n], conv_ps[b][:, 0:n], ACT.Copy,
                               scale=y_scale[:]).then_inc(y_scaled[b], 1)

            def step(j, k, load, bring, stats, weigh, conv):
                if weigh:
                    sign(j, k + 1, 2, 1)
                    sign(j, k + 1, 0, 0)
                if conv:
                    scale_out(j, k, 0)
                if weigh:
                    sign(j, k + 1, 0, 1)
                if conv:
                    scale_out(j, k, 1)
                if stats:
                    take_root(j, k)
                if bring:
                    copy_in(j, k, 0)
                if stats:
                    act.wait_ge(thr_ready, 3 * (4 * j + k + 3))
                    if not (isinstance(j, int) and 4 * j + k < 0):
                        act.wait_ge(hi_made, 4 * j + k + 1)
                        act.wait_ge(lo_made, 4 * j + k + 1)
                    sign(j, k + 2, 1, 0)
                if conv:
                    scale_out(j, k, 2)
                if bring:
                    copy_in(j, k, 1)
                if stats:
                    sign(j, k + 2, 1, 1)
                if conv:
                    scale_out(j, k, 3)
                if bring:
                    copy_in(j, k, 2)
                    copy_in(j, k, 3)
                if stats:
                    sign(j, k + 2, 2, 0)

            act.wait_ge(w_var_ready, 1)
            act.activation(w_stat[:, 5:6], w_stat[:, 4:5], ACT.Sqrt).then_inc(w_root_ready, 1)
            step(0, -3, **stages(-3))
            act.wait_ge(w_bias_ready, M_FIL)
            for m in range(M_FIL):
                act.activation(filt[:, m], w_raw[:], ACT.Sign, bias=w_bias[:, m:m + 1]).then_inc(w_signed, 1)
            act.wait_ge(consts_ready, 1)
            for k in (-2, -1):
                step(0, k, **stages(k))
            main_steps(act, step)

        @block.vector
        def _(dve):
            done = {"n": 0, "base": 0}

            def mark(ins):
                ins.then_inc(vec, 1)
                done["n"] += 1

            def settle():
                dve.wait_ge(vec, done["base"] + done["n"])

            def link(ins):
                mark(ins)
                settle()

            tt, ts, stt = nc.vector.tensor_tensor, nc.vector.tensor_scalar, nc.vector.scalar_tensor_tensor

            nc.vector.memset(w_raw[0:C, :, 1, :], 0.0)
            nc.vector.memset(w_raw[3 * C:4 * C, :, 0, :], 0.0)
            mark(nc.vector.memset(gram_lane[:], 0.0))
            for i in range(2):
                mark(nc.vector.memset(lane_stats[i][:], 1.0))
            nc.vector.memset(ones[:], 1.0)
            nc.vector.memset(eps_col[:], GN_EPS).then_inc(consts_ready, 1)
            dve.wait_ge(ident_ready, 1)
            mark(nc.vector.reduce_sum(own_group[:], ident[:].rearrange("p (g c) -> p g c", g=G), axis=AX.X))
            link(nc.vector.reduce_sum(same_ch_row[:], ident[:].rearrange("p (g c) -> p c g", g=G), axis=AX.X))
            nc.vector.tensor_copy(same_ch[:], same_ch_row[:].unsqueeze(1).broadcast_to([128, G, C]))\
                .then_inc(same_ch_ready, 1)

            def filter_lanes():
                dve.wait_ge(w_loaded, 32)
                link(nc.vector.bn_stats(w_stat[0:96, 6:12], w_raw[0:96, :, 0, :]))
                link(nc.vector.bn_aggr(w_stat[0:96, 0:2], w_stat[0:96, 6:12]))
                link(tt(w_stat[0:96, 2:3], w_stat[0:96, 0:1], w_stat[0:96, 0:1], ALU.mult))
                tt(w_stat[0:96, 1:2], w_stat[0:96, 1:2], w_stat[0:96, 2:3], ALU.add).then_inc(w_lane_stats, 1)
                mark(nc.vector.tensor_copy(filt[:, M_FIL], w_raw[:]))

            def filter_var():
                dve.wait_ge(w_summed, 1)
                link(ts(w_stat[:, 12:14], w_ps[:, 0:2], 1.0 / 96, None, ALU.mult))
                link(tt(w_stat[:, 3:4], w_stat[:, 12:13], w_stat[:, 12:13], ALU.mult))
                tt(w_stat[:, 4:5], w_stat[:, 13:14], w_stat[:, 3:4], ALU.subtract).then_inc(w_var_ready, 1)

            def filter_bias():
                dve.wait_ge(w_root_ready, 1)
                dve.wait_ge(w_var_ready, 1)
                link(nc.vector.reciprocal(w_stat[:, 14:15], w_stat[:, 5:6]))
                link(tt(w_stat[:, 14:15], w_stat[:, 14:15], w_stat[:, 4:5], ALU.mult))
                link(tt(w_stat[:, 15:16], w_stat[:, 14:15], w_stat[:, 5:6], ALU.add))
                for m in range(M_FIL):
                    u = -1.0 + m * 2.0 / (M_FIL - 1)
                    stt(w_bias[:, m:m + 1], w_stat[:, 15:16], 0.5 * u, w_stat[:, 12:13],
                        ALU.mult, ALU.subtract).then_inc(w_bias_ready, 1)

            def order_beta():
                link(stt(magn[:], params[:, 0, :], -1.0, params[:, 0, :], ALU.mult, ALU.max))
                mark(nc.vector.tensor_copy(tmp[:, 1, :], params[:, 0, :]))
                mark(ts(tmp[:, 2, :], params[:, 1, :], 0.5, 0.5, ALU.subtract, ALU.mult))
                mark(tt(tmp[:, 0, 1:2], magn[:, 1:2], magn[:, 2:3], ALU.is_ge))
                link(tt(tmp[:, 0, 0:1], magn[:, 1:2], magn[:, 2:3], ALU.max))
                link(tt(pick[:, 0, 0:1], magn[:, 0:1], tmp[:, 0, 0:1], ALU.is_ge))
                link(ts(pick[:, 1, 0:1], pick[:, 0, 0:1], -1.0, 1.0, ALU.mult, ALU.add))
                link(tt(pick[:, 0, 1:2], tmp[:, 0, 1:2], pick[:, 1, 0:1], ALU.mult))
                link(tt(pick[:, 0, 2:3], pick[:, 1, 0:1], pick[:, 0, 1:2], ALU.subtract))
                link(ts(pick[:, 1, 1:3], pick[:, 0, 1:3], -1.0, 1.0, ALU.mult, ALU.add))
                src = tmp[:, 1:3, :]
                mark(tt(tmp[:, 3:5, :], src, pick[:, 0:1, :].broadcast_to([128, 2, N_ACT]), ALU.mult))
                mark(tt(tmp[:, 5:7, 0:2], src[:, :, 1:3], pick[:, 1:2, 1:3].broadcast_to([128, 2, 2]), ALU.mult))
                link(tt(tmp[:, 7:9, 0:2], src[:, :, 0:1].broadcast_to([128, 2, 2]),
                        pick[:, 0:1, 1:3].broadcast_to([128, 2, 2]), ALU.mult))
                mark(nc.vector.reduce_sum(order[:, :, 0], tmp[:, 3:5, :], axis=AX.X))
                link(tt(order[:, :, 1:3], tmp[:, 5:7, 0:2], tmp[:, 7:9, 0:2], ALU.add))

            def split_ratios():
                link(ts(tmp[:, 5, 0:1], order[:, 0, 0:1], 0.0, None, ALU.is_equal))
                link(tt(tmp[:, 5, 1:2], tmp[:, 5, 0:1], order[:, 0, 0:1], ALU.add))
                link(nc.vector.reciprocal(tmp[:, 5, 2:3], tmp[:, 5, 1:2]))
                link(ts(tmp[:, 6, 0:2], order[:, 0, 1:3], tmp[:, 5, 2:3], None, ALU.mult))
                link(ts(tmp[:, 7, 0:2], tmp[:, 6, 0:2], GRID, ROUND, ALU.mult, ALU.add))
                link(ts(ratio_hi[:], tmp[:, 7, 0:2], ROUND, 1.0 / GRID, ALU.subtract, ALU.mult))
                link(tt(tmp[:, 3, 0:2], tmp[:, 6, 0:2], ratio_hi[:], ALU.subtract))
                ts(ratio_lo[:], tmp[:, 3, 0:2], LO_SCALE, None, ALU.mult).then_inc(ratios_ready, 1)

            def filter_gram():
                dve.wait_ge(w_signed, M_FIL)
                for m in range(M_FIL):
                    n = M_FIL + 1 - m
                    me = filt[0:96, m, :, 0, :]
                    link(tt(prod[:, m:], filt[0:96, m:, :, 0, :], me.unsqueeze(1).broadcast_to([96, n, TAPS, C]),
                            ALU.mult))
                    last = nc.vector.reduce_sum(gram_lane[:, m, m:], prod[:, m:].rearrange("p m a c -> p m (a c)"),
                                                axis=AX.X)
                    if m < M_FIL - 1:
                        link(last)
                last.then_inc(gram_lanes, 1)

            def filter_solve():
                dve.wait_ge(gram_summed, 1)
                link(nc.vector.tensor_copy(gram[:], w_ps[:, 0:30].rearrange("p (m n) -> p m n", m=M_FIL)))
                for m in range(M_FIL):
                    link(nc.vector.reciprocal(inv[:, 0:1], gram[:, m, m:m + 1]))
                    link(ts(neg_row[:, m, m:], gram[:, m, m:], inv[:, 0:1], -1.0, ALU.mult, ALU.mult))
                    r = M_FIL - 1 - m
                    if r:
                        col = gram[:, m, m + 1:M_FIL].unsqueeze(2).broadcast_to([128, r, r + 1])
                        row = neg_row[:, m, m + 1:].unsqueeze(1).broadcast_to([128, r, r + 1])
                        link(tt(outer[:, m + 1:, m + 1:], col, row, ALU.mult))
                        link(tt(gram[:, m + 1:, m + 1:], gram[:, m + 1:, m + 1:], outer[:, m + 1:, m + 1:], ALU.add))
                link(ts(alpha[:], neg_row[:, :, M_FIL], -1.0, None, ALU.mult))
                for m in range(M_FIL - 1, 0, -1):
                    link(stt(alpha[:, 0:m], neg_row[:, 0:m, m], alpha[:, m:m + 1], alpha[:, 0:m], ALU.mult, ALU.add))

            def filter_parts():
                flat_w = w_eff[:].rearrange("p a o c -> p (a o c)")
                fl = [filt[:, m].rearrange("p a o c -> p (a o c)") for m in range(M_FIL)]
                mark(stt(w_stat[:, 6:11], alpha[:], -1.0, alpha[:], ALU.mult, ALU.max))
                link(ts(flat_w, fl[0], alpha[:, 0:1], None, ALU.mult))
                mark(nc.vector.reduce_sum(inv[:, 1:2], w_stat[:, 6:11], axis=AX.X))
                for m in range(1, M_FIL):
                    link(stt(flat_w, fl[m], alpha[:, m:m + 1], flat_w, ALU.mult, ALU.add))
                    if m == 1:
                        mark(nc.vector.reciprocal(inv[:, 2:3], inv[:, 1:2]))
                link(ts(flat_w, flat_w, inv[:, 2:3], W_SCALE, ALU.mult, ALU.mult))
                wm = [w_mm[:, i].rearrange("p a o c -> p (a o c)") for i in range(3)]
                link(nc.vector.tensor_copy(wm[0], flat_w))
                mark(tt(wm[1], flat_w, wm[0], ALU.subtract))
                link(ts(wm[2], wm[0], 1.0 / LO_SCALE, None, ALU.mult))
                mark(nc.vector.memset(w_mm[0:C, :, :, 1, :], 0.0))
                mark(nc.vector.memset(w_mm[3 * C:4 * C, :, :, 0, :], 0.0))
                mark(ts(y_scale[:], inv[:, 1:2], order[:, 0, 0:1], 1.0 / W_SCALE, ALU.mult, ALU.mult))
                mark(nc.vector.reduce_sum(w_stat[:, 0:1], alpha[:], axis=AX.X))
                link(tt(tmp[:, 0, :], params[:, 0, :], params[:, 2, :], ALU.mult))
                link(nc.vector.reduce_sum(w_stat[:, 1:2], tmp[:, 0, :], axis=AX.X))
                tt(y_const[:], w_stat[:, 0:1], w_stat[:, 1:2], ALU.mult).then_inc(w_ready, 1)
                dve.wait_ge(w_ready, 1)

            def flat(b, n):
                return signs[b][:, n].rearrange("p i a h -> p (i a h)")

            def rows(t):
                return t.rearrange("p (r h) -> p r h", h=H)

            def add_x(j, k, c):
                b, _ = place(j, k, 2)
                s, _ = place(j, k, UNROLL)
                dve.wait_ge(y_transposed, OPEN + CHUNKS * (4 * j + k) + c + 1)
                lo, hi = max(16 * c - 1, 0), min(16 * c + 15, W)
                off = C if c == 0 else 0
                stt(y_nat[b][:, C * lo:C * hi], y_ps[c % 2][0:ROWS, off:off + C * (hi - lo)],
                    y_const[0:ROWS, :], x_nat[s][:, C * lo:C * hi],
                    ALU.add, ALU.add).then_inc(y_added[c % 2], 1)

            def lane_moments(j, k, half):
                b, _ = place(j, k, 2)
                for i in range(2):
                    dve.wait_ge(x_copied[i], 2 * (4 * j + k) + half + 1)
                for a in range(2):
                    mark(nc.vector.bn_stats(raw_stats[b][:, a, half, :],
                                            x_ch[b][:, a, 7 * half:7 * half + 7, :].rearrange("p i h -> p (i h)")))

            def step(j, k, load, bring, stats, weigh, conv):
                p = 4 * j + k
                q, r = p + 2, p + 1
                qb, rb = (k + 2) % 2, (k + 1) % 2
                if stats:
                    lane_moments(j, k + 2, 1)
                    settle()
                if weigh:
                    dve.wait_ge(signed, 6 * r + 2)
                    mark(ts(part1[:], flat(rb, 1), ratio_hi[:, 0:1], None, ALU.mult))
                if stats:
                    for a in range(2):
                        mark(nc.vector.bn_aggr(lane_stats[qb][:, a, 1:3],
                                               raw_stats[qb][:, a].rearrange("p i s -> p (i s)")))
                    settle()
                    tt(spread_stats[qb][:], own_group[:].unsqueeze(2).broadcast_to([128, G, 6]),
                       lane_stats[qb][:].rearrange("p a s -> p (a s)").unsqueeze(1).broadcast_to([128, G, 6]),
                       ALU.mult).then_inc(lanes_ready, 1)
                if weigh:
                    dve.wait_ge(signed, 6 * r + 4)
                if stats:
                    dve.wait_ge(gathered, q + 1)
                if weigh:
                    mark(ts(part2[:], flat(rb, 2), ratio_hi[:, 1:2], None, ALU.mult))
                if stats:
                    st = stat_ps[:, 0:G * 6].rearrange("p (g a s) -> p g a s", g=G, a=2)
                    for a in range(2):
                        nc.vector.bn_aggr(moments[qb][:, a, :], st[:, :, a, :]).then_inc(moments_ready, 1)
                    dve.wait_ge(moments_ready, 2 * (q + 1))
                    mark(ts(var_eps[:], moments[qb][:, :, 1], GN_EPS, None, ALU.add))
                if weigh:
                    settle()
                    mark(tt(half_hi[:], part1[:], part2[:], ALU.add))
                    settle()
                    dve.wait_ge(signed, 6 * (r + 1))
                    if conv:
                        dve.wait_ge(conv_done, OPEN + CHUNKS * (r - 1))
                    else:
                        dve.wait_ge(pads_ready, 4)
                    tt(s_even[rb][:, 0, :].rearrange("p (r h) -> p r h", h=HP)[:, :, 1:1 + H], rows(half_hi[:]),
                       signs[rb][:, 0].rearrange("p i a h -> p (i a) h"), ALU.add).then_inc(hi_made, 1)
                if stats:
                    dve.wait_ge(root_ready, q + 1)
                    mark(nc.vector.reciprocal(inv_root[:], root[:]))
                    settle()
                    mark(tt(twice_dev[:], var_eps[:], inv_root[:], ALU.mult))
                    settle()
                    mark(tt(twice_dev[:], twice_dev[:], root[:], ALU.add))
                    settle()
                    for n in range(N_ACT):
                        stt(neg_thr[qb][:, n, :], twice_dev[:], order[:, 1, n:n + 1], moments[qb][:, :, 0],
                            ALU.mult, ALU.subtract).then_inc(thr_ready, 1)
                if conv:
                    dve.wait_ge(y_stored[k % 2], 16 * (OPEN + 4 * j + 2 * (k // 2)))
                    add_x(j, k, 0)
                    add_x(j, k, 1)
                if bring:
                    lane_moments(j, k + AHEAD, 0)
                if conv:
                    add_x(j, k, 2)
                    add_x(j, k, 3)

            filter_lanes()
            dve.wait_ge(params_loaded, 48)
            order_beta()
            filter_var()
            split_ratios()
            filter_bias()
            step(0, -3, **stages(-3))
            step(0, -2, **stages(-2))
            filter_gram()
            step(0, -1, **stages(-1))
            filter_solve()
            filter_parts()

            start = done["n"]
            with dve.Fori(0, LOOP) as j:
                done["base"] = UNROLL * MARKS_PER_STEP * j
                for k in range(UNROLL):
                    step(j, k, **FULL)
                assert done["n"] - start == UNROLL * MARKS_PER_STEP, (done["n"] - start) / UNROLL
            done["base"], done["n"] = 0, start + UNROLL * MARKS_PER_STEP * LOOP
            for k in range(UNROLL):
                step(LOOP, k, **stages(UNROLL * LOOP + k))

        @block.tensor
        def _(pe):
            def bring_in(j, k, c):
                q = k + AHEAD
                s, uses = place(j, q, UNROLL)
                if c == 0:
                    pe.wait_ge(x_loaded[s], 16 * (uses + 1))
                if not (isinstance(j, int) and 4 * j + q == 0 and c < 2):
                    pe.wait_ge(x_copied[c % 2], 2 * (4 * j + q) + c // 2)
                for i in range(CB[c]):
                    blk = 4 * c + i
                    last = nc.tensor.transpose(x_ps[c % 2][:, i * ROWS:(i + 1) * ROWS],
                                               x_nat[s][:, 128 * blk:128 * (blk + 1)], ident[0:ROWS, 0:ROWS])
                last.then_inc(x_transposed, 1)

            def gather_lanes(j, k):
                q = 4 * j + k + 2
                b, _ = place(j, k + 2, 2)
                pe.wait_ge(lanes_ready, q + 1)
                if not (isinstance(j, int) and q == 0):
                    pe.wait_ge(moments_ready, 2 * q)
                nc.tensor.matmul(stat_ps[:, 0:6 * G], same_ch[:].rearrange("p g c -> p (g c)"),
                                 spread_stats[b][:].rearrange("p g s -> p (g s)"),
                                 start=True, stop=True).then_inc(gathered, 1)

            PRODUCTS = [(0, 0), (0, 1), (1, 2)]

            def convolve(j, k, c, stats=False):
                b, uses = place(j, k, 2)
                bank = c % 2
                pe.wait_ge(y_scaled[bank], OPEN + 2 * (4 * j + k) + c // 2)
                even = s_even[b][:].rearrange("p s (r h) -> p s r h", h=HP)
                odd = s_odd[b][:].rearrange("p s (r h) -> p s r h", h=HP)
                for n, (part, kind) in enumerate(PRODUCTS):
                    if n == 1 and stats:
                        gather_lanes(j, k)
                    if c == 0 and n in (0, 2):
                        made, shifted = ((hi_made, shifted_hi), (lo_made, shifted_lo))[part]
                        pe.wait_ge(made, 4 * j + k + 1)
                        pe.wait_ge(shifted[b], 32 * (uses + 1))
                    for t in range(TAPS):
                        first, end = n == 0 and t == 0, n == 2 and t == TAPS - 1
                        wt = w_mm[:, kind, t].rearrange("p o c -> p (o c)")
                        r0 = 2 * 4 * c
                        nc.tensor.matmul(conv_ps[bank][0:64, 0:CO[c] * ROWS], wt,
                                         odd[:, part, r0:r0 + 2 * CO[c], t:t + H], start=first, stop=end)
                        last = nc.tensor.matmul(conv_ps[bank][64:128, 0:CB[c] * ROWS], wt,
                                                even[:, part, r0:r0 + 2 * CB[c], t:t + H], start=first, stop=end)
                last.then_inc(conv_done, 1)

            def bring_out(j, k, c):
                bank = c % 2
                pe.wait_ge(y_scaled[bank], OPEN + 2 * (4 * j + k) + c // 2 + 1)
                pe.wait_ge(y_added[bank], OPEN + 2 * (4 * j + k) + c // 2)
                for i in range(CO[c]):
                    p = 128 if i < CB[c] else C
                    last = nc.tensor.transpose(y_ps[bank][0:ROWS, 128 * i:128 * i + p],
                                               y_ch[bank][0:p, i * ROWS:(i + 1) * ROWS], ident[0:p, 0:p])
                last.then_inc(y_transposed, 1)

            def step(j, k, load, bring, stats, weigh, conv):
                if conv:
                    convolve(j, k, 0)
                    convolve(j, k, 1, stats)
                elif stats:
                    gather_lanes(j, k)
                if bring:
                    bring_in(j, k, 0)
                if conv:
                    bring_out(j, k, 0)
                    convolve(j, k, 2)
                if bring:
                    bring_in(j, k, 1)
                if conv:
                    bring_out(j, k, 1)
                    convolve(j, k, 3)
                if bring:
                    bring_in(j, k, 2)
                if conv:
                    bring_out(j, k, 2)
                if bring:
                    bring_in(j, k, 3)
                if conv:
                    bring_out(j, k, 3)

            pe.wait_ge(w_lane_stats, 1)
            pe.wait_ge(consts_ready, 1)
            nc.tensor.matmul(w_ps[:, 0:2], ones[0:96, :], w_stat[0:96, 0:2], start=True, stop=True)\
                .then_inc(w_summed, 1)
            pe.wait_ge(ident_ready, 1)
            step(0, -3, **stages(-3))
            pe.wait_ge(same_ch_ready, 1)
            step(0, -2, **stages(-2))
            pe.wait_ge(gram_lanes, 1)
            nc.tensor.matmul(w_ps[:, 0:30], ones[0:96, :], gram_lane[:].rearrange("p m n -> p (m n)"),
                             start=True, stop=True).then_inc(gram_summed, 1)
            step(0, -1, **stages(-1))
            pe.wait_ge(w_ready, 1)
            main_steps(pe, step)


MARKS_PER_STEP = 13


_INS = ["x", "L0_conv_W", "L0_conv_beta", "L0_conv_v", "L0_conv_bias"]


def kernel(**inputs):
    import numpy as np
    import concourse.bacc as bacc
    from concourse.bass_utils import run_bass_kernel_spmd

    nc = bacc.Bacc("TRN2", target_bir_lowering=False, num_devices=1)
    arrays, args = {}, []
    for name in _INS:
        a = np.ascontiguousarray(inputs[name])
        arrays[f"in_{name}"] = a
        args.append(nc.dram_tensor(f"in_{name}", a.shape, mybir.dt.from_np(a.dtype), kind="ExternalInput").ap())
    out = nc.dram_tensor("out_0", inputs["x"].shape, FP32, kind="ExternalOutput").ap()
    preact_conv_kernel(nc, *args, out)
    r = run_bass_kernel_spmd(nc, [arrays], core_ids=[0])
    return r.results[0]["out_0"]
```

```python
from contextlib import ExitStack

import concourse.bass as bass
from concourse import mybir

FP32 = mybir.dt.float32
FP16 = mybir.dt.float16
ALU = mybir.AluOpType
ACT = mybir.ActivationFunctionType
AX = mybir.AxisListType

IMAGES, H, W, C = 32, 56, 56, 32
TAPS = 3
N_ACT = 3
M_FIL = 5
PAIRS = IMAGES // 2
ROWS = 2 * H
G = 4
BLOCKS = W // G
POS = BLOCKS * ROWS
HP = H + 2
BLK = 2 * HP
CHUNKS = 4
CB = [4, 4, 4, 2]
BANK = 512
UNROLL = 4
AHEAD = 3
GRID = 2.0 ** 9
LO_SCALE = 2.0 ** 10
W_SCALE = 2.0 ** 10
ROUND = 1.5 * 2.0 ** 23
GN_EPS = 1e-5
GC = C // 2
GP = GC * (M_FIL + 1)


def preact_conv_kernel(nc, x, w, beta, v, bias, out):
    ctx = ExitStack()
    with ctx:
        def sb(name, shape, dt=FP32):
            return ctx.enter_context(nc.sbuf_tensor(name, shape, dt))

        def ps(name, shape):
            return ctx.enter_context(nc.psum_tensor(name, shape, FP32))

        def sem(name):
            return ctx.enter_context(nc.semaphore(name))

        x_nat = [sb(f"x_nat{i}", [ROWS, (1 + W) * C]) for i in range(UNROLL)]
        y_nat = [sb(f"y_nat{i}", [ROWS, W * C]) for i in range(2)]
        x_ch = [sb(f"x_ch{i}", [128, 2, BLOCKS, H]) for i in range(2)]
        signs = [sb(f"signs{i}", [128, N_ACT, BLOCKS, 2, H], FP16) for i in range(2)]
        hi_part = [sb(f"hi_part{n}", [128, POS], FP16) for n in (1, 2)]
        lo_part = [sb(f"lo_part{n}", [128, POS], FP16) for n in (1, 2)]
        half_hi = sb("half_hi", [128, POS], FP16)
        s_even = [sb(f"s_even{i}", [128, 2, (BLOCKS + 1) * BLK], FP16) for i in range(2)]
        s_odd = [sb(f"s_odd{i}", [128, 2, BLOCKS * BLK], FP16) for i in range(2)]
        y_ch = [sb(f"y_ch{i}", [128, 4 * ROWS]) for i in range(2)]
        raw_stats = [sb(f"raw_stats{i}", [128, 2, 2, 6]) for i in range(2)]
        lane_stats = [sb(f"lane_stats{i}", [128, 2, 3]) for i in range(2)]
        spread_stats = [sb(f"spread_stats{i}", [128, G, 6]) for i in range(2)]
        moments = [sb(f"moments{i}", [128, 2, 2]) for i in range(2)]
        root = sb("root", [128, 2])
        inv_root = sb("inv_root", [128, 2])
        twice_dev = sb("twice_dev", [128, 2])
        neg_thr = [sb(f"neg_thr{i}", [128, N_ACT, 2]) for i in range(2)]
        ident = sb("ident", [128, 128])
        own_group = sb("own_group", [128, G])
        same_ch = sb("same_ch", [128, G, C])
        same_ch_row = sb("same_ch_row", [128, C])
        wait_carrier = sb("wait_carrier", [128, 2, 2])
        dve_carrier = sb("dve_carrier", [128, 1])
        opening = sb("opening", [128, 8])
        ones = sb("ones", [128, 128])
        eps_col = sb("eps_col", [128, 1])
        params = sb("params", [128, 3, N_ACT])
        beta_bias = sb("beta_bias", [128, N_ACT])
        magn = sb("magn", [128, N_ACT])
        pick = sb("pick", [128, 2, N_ACT])
        order = sb("order", [128, 2, N_ACT])
        tmp = sb("tmp", [128, 9, N_ACT])
        ratio_hi = sb("ratio_hi", [128, 2])
        ratio_lo = sb("ratio_lo", [128, 2])
        w_raw = sb("w_raw", [128, TAPS, 2, C])
        filt = sb("filt", [128, TAPS, 2, C, M_FIL + 1])
        gram_prod = sb("gram_prod", [GP, M_FIL + 1, GC])
        w_stat = sb("w_stat", [128, 16])
        w_bias = sb("w_bias", [128, M_FIL])
        gram_lane = sb("gram_lane", [GP, M_FIL + 1])
        gram_spread = sb("gram_spread", [GP, M_FIL, M_FIL + 1])
        own_filter = sb("own_filter", [GP, M_FIL])
        same_col = sb("same_col", [GP, GC])
        gram = sb("gram", [128, M_FIL, M_FIL + 1])
        outer = sb("outer", [128, M_FIL, M_FIL + 1])
        neg_row = sb("neg_row", [128, M_FIL, M_FIL + 1])
        inv = sb("inv", [128, M_FIL])
        size = sb("size", [128, 3])
        w_eff = sb("w_eff", [128, TAPS, 2, C])
        w_mm = sb("w_mm", [128, 3, TAPS, 2, C], FP16)
        y_scale = sb("y_scale", [128, 1])
        y_const = sb("y_const", [128, 1])

        x_ps = [ps(f"x_ps{i}", [128, BANK]) for i in range(2)]
        conv_ps = [ps(f"conv_ps{i}", [128, BANK]) for i in range(2)]
        y_ps = [ps(f"y_ps{i}", [128, BANK]) for i in range(2)]
        stat_ps = ps("stat_ps", [128, BANK])
        w_ps = ps("w_ps", [128, BANK])

        x_loaded = [[sem(f"x_{half}_loaded{i}") for i in range(UNROLL)] for half in ("left", "right")]
        x_transposed = sem("x_transposed")
        x_copied = [sem(f"x_copied{i}") for i in range(2)]
        lanes_ready = sem("lanes_ready")
        gathered = sem("gathered")
        moments_ready = sem("moments_ready")
        root_ready = sem("root_ready")
        thr_ready = sem("thr_ready")
        signed = sem("signed")
        hi_made, lo_made = sem("hi_made"), sem("lo_made")
        shifted_hi = [sem(f"shifted_hi{i}") for i in range(2)]
        shifted_lo = [sem(f"shifted_lo{i}") for i in range(2)]
        conv_done = sem("conv_done")
        y_scaled = [sem(f"y_scaled{i}") for i in range(2)]
        y_transposed = sem("y_transposed")
        y_added = [sem(f"y_added{i}") for i in range(2)]
        y_stored = [sem(f"y_stored{i}") for i in range(2)]
        last_stored = sem("last_stored")
        ident_zero, ident_ready = sem("ident_zero"), sem("ident_ready")
        same_ch_ready = sem("same_ch_ready")
        pads_ready = sem("pads_ready")
        order_ready = sem("order_ready")
        ratios_ready = sem("ratios_ready")
        divisor_ready, inverse_ready = sem("divisor_ready"), sem("inverse_ready")
        pool_vec = sem("pool_vec")
        params_loaded = sem("params_loaded")
        bias_loaded = sem("bias_loaded")
        w_loaded = sem("w_loaded")
        consts_ready = sem("consts_ready")
        w_lane_stats = sem("w_lane_stats")
        w_summed = sem("w_summed")
        w_var_ready = sem("w_var_ready")
        w_root_ready = sem("w_root_ready")
        w_bias_ready = sem("w_bias_ready")
        w_signed = sem("w_signed")
        w_copied = sem("w_copied")
        corners_zero = sem("corners_zero")
        gram_made = sem("gram_made")
        gram_lanes = sem("gram_lanes")
        gram_summed = sem("gram_summed")
        w_ready = sem("w_ready")
        y_scale_ready = sem("y_scale_ready")
        hi_part1_made = sem("hi_part1_made")
        vec = sem("vec")
        lo_parts = sem("lo_parts")

        x_pairs = x.rearrange("(n a) h w c -> n (a h) (w c)", a=2)
        out_pairs = out.rearrange("(n a) h w c -> n (a h) (w c)", a=2)

        OPEN = 1

        def place(j, k, depth):
            return k % depth, (UNROLL // depth) * j + k // depth

        def stages(k0):
            return dict(load=k0 + UNROLL < PAIRS and k0 >= 0, bring=k0 + AHEAD < PAIRS,
                        stats=0 <= k0 + 2 < PAIRS, weigh=0 <= k0 + 1 < PAIRS, conv=k0 >= 0)

        WARM = 10
        HALF = C * 32
        HALVES = [slice(0, HALF), slice(HALF, W * C)]
        LAST = C * 48
        GRAM = slice(128, 128 + M_FIL * (M_FIL + 1))
        LOOP = 3
        FULL = dict(load=True, bring=True, stats=True, weigh=True, conv=True)

        def main_steps(eng, step):
            with eng.Fori(0, LOOP) as j:
                for k in range(UNROLL):
                    step(j, k, **FULL)
            for k in range(UNROLL):
                step(LOOP, k, **stages(UNROLL * LOOP + k))

        REGIONS = [(0, C, 0, 1, BLOCKS), (C, 2 * C, 0, 1, 0), (2 * C, 4 * C, 0, 1, 0),
                   (0, 4 * C, 1, BLOCKS, 1)]

        def window_rows(b, part, region):
            p0, p1, i0, i1, at = region
            return s_even[b][p0:p1, part, :].rearrange("p (r h) -> p r h", h=HP)[
                :, 2 * at:2 * (at + i1 - i0), 1:1 + H]

        def block_rows(t, region):
            p0, p1, i0, i1, _ = region
            return t[p0:p1, i0 * ROWS:i1 * ROWS].rearrange("p (r h) -> p r h", h=H)

        def load_filter(eng, o):
            eng.dma_start(w_raw[C * o:C * (o + TAPS), :, o, :], w.rearrange("a k i o -> (k i) a o"))\
                .then_inc(w_loaded, 16)

        block = ctx.enter_context(nc.Block())

        @block.sync
        def _(sp):
            def load_x(j, k, half):
                s, _ = place(j, k, UNROLL)
                cols = HALVES[half]
                sp.dma_start(x_nat[s][:, C + cols.start:C + cols.stop], x_pairs[4 * j + k][:, cols])\
                    .then_inc(x_loaded[half][s], 16)
                if half == 0:
                    sp.dma_start(x_nat[s][:, 0:C], x_pairs[4 * j + k][:, (W - 1) * C:])\
                        .then_inc(x_loaded[half][s], 16)

            load_filter(sp, 0)
            load_x(0, 0, 0)
            load_x(0, 0, 1)
            sp.dma_start(params[:, 1, :], v.partition_broadcast(128)).then_inc(params_loaded, 16)
            for k in range(1, UNROLL):
                load_x(0, k, 0)
                load_x(0, k, 1)
            sp.dma_start(params[:, 2, :], bias.partition_broadcast(128)).then_inc(bias_loaded, 16)

            def step(j, k, load, bring, stats, weigh, conv):
                if weigh:
                    b, uses = place(j, k + 1, 2)
                    for part, made, shifted in ((0, hi_made, shifted_hi), (1, lo_made, shifted_lo)):
                        sp.wait_ge(made, 4 * j + k + 2)
                        sp.dma_start(s_odd[b][0:64, part, :], s_even[b][64:128, part, 0:BLOCKS * BLK])\
                            .then_inc(shifted[b], 16)
                        sp.dma_start(s_odd[b][64:128, part, :], s_even[b][0:64, part, BLK:])\
                            .then_inc(shifted[b], 16)
                if conv:
                    last_pair = isinstance(j, int) and 4 * j + k == PAIRS - 1
                    b, uses = place(j, k, 2)
                    for half, cols in enumerate(HALVES):
                        if last_pair and half == 1:
                            sp.wait_ge(y_added[0], OPEN + 2 * (4 * j + k) + half + 1)
                            sp.dma_start(out_pairs[4 * j + k][:, HALF:LAST], y_nat[b][:, HALF:LAST])\
                                .then_inc(last_stored, 16)
                            cols = slice(LAST, W * C)
                        sp.wait_ge(y_added[1], OPEN + 2 * (4 * j + k) + half + 1)
                        if load:
                            load_x(j, k + UNROLL, half)
                        sp.dma_start(out_pairs[4 * j + k][:, cols], y_nat[b][:, cols]).then_inc(y_stored[b], 16)

            step(0, -1, **stages(-1))
            main_steps(sp, step)
            for b in range(2):
                sp.wait_ge(y_stored[b], 16 * (OPEN + PAIRS))
            sp.wait_ge(last_stored, 16)

        @block.gpsimd
        def _(pool):
            pool.memset(ident[:], 0.0).then_inc(ident_zero, 1)
            pool.wait_ge(ident_zero, 1)
            pool.affine_select(out=ident[:], in_=ident[:], compare_op=ALU.not_equal, fill=1.0, base=0,
                               pattern=[[-1, 128]], channel_multiplier=1).then_inc(ident_ready, 1)

            tt, ts = nc.gpsimd.tensor_tensor, nc.gpsimd.tensor_scalar
            done = {"n": 0}

            def mark(ins):
                ins.then_inc(pool_vec, 1)
                done["n"] += 1

            def link(ins):
                mark(ins)
                pool.wait_ge(pool_vec, done["n"])

            def order_beta():
                pool.wait_ge(params_loaded, 32)
                mark(nc.gpsimd.tensor_copy(tmp[:, 1, :], params[:, 0, :]))
                mark(ts(tmp[:, 2, :], params[:, 1, :], 0.5, 0.5, ALU.subtract, ALU.mult))
                for n in range(N_ACT):
                    link(ts(magn[:, n:n + 1], params[:, 0, n:n + 1], -1.0, params[:, 0, n:n + 1], ALU.mult, ALU.max))
                mark(ts(tmp[:, 0, 1:2], magn[:, 1:2], magn[:, 2:3], 1.0, ALU.is_ge, ALU.mult))
                mark(ts(tmp[:, 0, 0:1], magn[:, 0:1], magn[:, 1:2], 1.0, ALU.is_ge, ALU.mult))
                link(ts(tmp[:, 0, 2:3], magn[:, 0:1], magn[:, 2:3], 1.0, ALU.is_ge, ALU.mult))
                link(tt(pick[:, 0, 0:1], tmp[:, 0, 0:1], tmp[:, 0, 2:3], ALU.mult))
                link(ts(pick[:, 1, 0:1], pick[:, 0, 0:1], -1.0, 1.0, ALU.mult, ALU.add))
                link(tt(pick[:, 0, 1:2], tmp[:, 0, 1:2], pick[:, 1, 0:1], ALU.mult))
                link(tt(pick[:, 0, 2:3], pick[:, 1, 0:1], pick[:, 0, 1:2], ALU.subtract))
                link(ts(pick[:, 1, 1:3], pick[:, 0, 1:3], -1.0, 1.0, ALU.mult, ALU.add))
                src = tmp[:, 1:3, :]
                mark(tt(tmp[:, 3:5, :], src, pick[:, 0:1, :].broadcast_to([128, 2, N_ACT]), ALU.mult))
                mark(tt(tmp[:, 5:7, 0:2], src[:, :, 1:3], pick[:, 1:2, 1:3].broadcast_to([128, 2, 2]), ALU.mult))
                link(tt(tmp[:, 7:9, 0:2], src[:, :, 0:1].broadcast_to([128, 2, 2]),
                        pick[:, 0:1, 1:3].broadcast_to([128, 2, 2]), ALU.mult))
                tt(order[:, :, 1:3], tmp[:, 5:7, 0:2], tmp[:, 7:9, 0:2], ALU.add).then_inc(order_ready, 1)
                tt(order[:, :, 0:1], tmp[:, 3:5, 0:1], tmp[:, 3:5, 1:2], ALU.add).then_inc(order_ready, 1)
                pool.wait_ge(order_ready, 2)
                tt(order[:, :, 0:1], order[:, :, 0:1], tmp[:, 3:5, 2:3], ALU.add).then_inc(order_ready, 1)
                pool.wait_ge(order_ready, 3)

            def split_ratios():
                link(ts(tmp[:, 5, 0:1], order[:, 0, 0:1], 0.0, 1.0, ALU.is_equal, ALU.mult))
                tt(tmp[:, 5, 1:2], tmp[:, 5, 0:1], order[:, 0, 0:1], ALU.add).then_inc(divisor_ready, 1)
                pool.wait_ge(inverse_ready, 1)
                link(ts(tmp[:, 6, 0:2], order[:, 0, 1:3], tmp[:, 5, 2:3], 1.0, ALU.mult, ALU.mult))
                link(ts(tmp[:, 7, 0:2], tmp[:, 6, 0:2], GRID, ROUND, ALU.mult, ALU.add))
                ts(ratio_hi[:], tmp[:, 7, 0:2], ROUND, 1.0 / GRID, ALU.subtract, ALU.mult).then_inc(ratios_ready, 1)
                pool.wait_ge(ratios_ready, 1)
                tt(ratio_lo[:], tmp[:, 6, 0:2], ratio_hi[:], ALU.subtract).then_inc(ratios_ready, 1)
                pool.wait_ge(ratios_ready, 2)
                ts(ratio_lo[:], ratio_lo[:], LO_SCALE, 1.0, ALU.mult, ALU.mult).then_inc(ratios_ready, 1)

            for i, (s, n) in enumerate([(conv_done, 1), (y_transposed, 1), (y_scaled[0], 1), (y_scaled[1], 1),
                                        (y_added[0], 1), (y_added[1], 1), (y_stored[0], 16), (y_stored[1], 16)]):
                pool.memset(opening[:, i:i + 1], 0.0).then_inc(s, n)
            for b in range(2):
                edge = s_even[b][:].rearrange("p s (r h) -> p (s r) h", h=HP)
                pool.memset(edge[:, :, 0], 0.0).then_inc(pads_ready, 1)
                pool.memset(edge[:, :, HP - 1], 0.0).then_inc(pads_ready, 1)
                col = s_even[b][:].rearrange("p s (r h) -> p s r h", h=HP)
                pool.memset(col[:, :, 0:2, 1:1 + H], 0.0).then_inc(pads_ready, 1)
                pool.memset(col[:, :, 2 * BLOCKS:, 1:1 + H], 0.0).then_inc(pads_ready, 1)
            pool.wait_ge(w_loaded, 32)
            pool.tensor_copy(filt[0:96, :, 0, :, M_FIL], w_raw[0:96, :, 0, :]).then_inc(w_copied, 1)
            order_beta()
            split_ratios()
            pool.wait_ge(ratios_ready, 3)
            pool.wait_ge(w_copied, 1)
            pool.wait_ge(w_signed, M_FIL)
            pool.memset(filt[0:C, :, 1, :, 0:M_FIL], 0.0).then_inc(corners_zero, 1)
            pool.memset(filt[3 * C:4 * C, :, 0, :, 0:M_FIL], 0.0).then_inc(corners_zero, 1)
            pool.wait_ge(corners_zero, 2)

            def step(j, k, load, bring, stats, weigh, conv):
                if not weigh:
                    return
                r = 4 * j + k + 1
                b, _ = place(j, k + 1, 2)
                if conv:
                    pool.wait_ge(lo_made, r)
                    pool.wait_ge(conv_done, OPEN + CHUNKS * (r - 1))
                else:
                    pool.wait_ge(pads_ready, 8)
                for n, part in ((1, lo_part[0]), (2, lo_part[1])):
                    pool.wait_ge(signed, 6 * r + 2 * n)
                    pool.tensor_tensor(wait_carrier[:, n - 1, :], ratio_lo[:], ratio_lo[:], ALU.add)
                    pool.tensor_scalar(part[:], signs[b][:, n].rearrange("p i a h -> p (i a h)"),
                                       ratio_lo[:, n - 1:n], 1.0, ALU.mult, ALU.mult).then_inc(lo_parts, 1)
                pool.wait_ge(lo_parts, 5 * r + 2)
                for i, region in enumerate(REGIONS):
                    if i == len(REGIONS) - 1:
                        pool.wait_ge(lo_parts, 5 * (r + 1))
                    pool.tensor_tensor(window_rows(b, 1, region), block_rows(lo_part[0], region),
                                       block_rows(lo_part[1], region), ALU.add)\
                        .then_inc(lo_made if i == len(REGIONS) - 1 else lo_parts, 1)

            step(0, -1, **stages(-1))
            main_steps(pool, step)

        @block.scalar
        def _(act):
            load_filter(act, 1)
            act.dma_start(params[:, 0, :], beta.partition_broadcast(128)).then_inc(params_loaded, 16)

            def copy_in(j, k, c):
                q = k + AHEAD
                b, _ = place(j, q, 2)
                if c == 0 and not (isinstance(j, int) and 4 * j + q < 2):
                    act.wait_ge(signed, 6 * (4 * j + q - 1))
                act.wait_ge(x_transposed, CHUNKS * (4 * j + q) + c + 1)
                n = CB[c]
                act.activation(x_ch[b][:, :, 4 * c:4 * c + n, :].rearrange("p a i h -> p i a h"),
                               x_ps[c % 2][:, 0:n * ROWS].rearrange("p (i a h) -> p i a h", a=2, h=H),
                               ACT.Copy).then_inc(x_copied[c % 2], 1)

            def sign(j, k, n, a):
                b, _ = place(j, k, 2)
                act.activation(signs[b][:, n, :, a, :], x_ch[b][:, a], ACT.Sign,
                               bias=neg_thr[b][:, n, a:a + 1]).then_inc(signed, 1)

            def take_root(j, k):
                b, _ = place(j, k + 2, 2)
                act.wait_ge(moments_ready, 2 * (4 * j + k + 3))
                act.activation(root[:], moments[b][:, :, 1], ACT.Sqrt, bias=eps_col[:]).then_inc(root_ready, 1)

            def scale_out(j, k, c):
                b = c % 2
                act.wait_ge(conv_done, OPEN + CHUNKS * (4 * j + k) + c + 1)
                act.wait_ge(y_transposed, OPEN + CHUNKS * (4 * j + k) + c - 1 if c else
                            OPEN + CHUNKS * (4 * j + k))
                n = CB[c] * ROWS
                act.activation(y_ch[b][:, 0:n], conv_ps[b][:, 0:n], ACT.Copy,
                               scale=y_scale[:]).then_inc(y_scaled[b], 1)

            def step(j, k, load, bring, stats, weigh, conv):
                if weigh:
                    sign(j, k + 1, 2, 1)
                    sign(j, k + 1, 0, 0)
                if conv:
                    scale_out(j, k, 0)
                if weigh:
                    sign(j, k + 1, 0, 1)
                if stats:
                    take_root(j, k)
                if conv:
                    scale_out(j, k, 1)
                if bring:
                    copy_in(j, k, 0)
                if stats:
                    act.wait_ge(thr_ready, 3 * (4 * j + k + 3))
                    if not (isinstance(j, int) and 4 * j + k < 0):
                        act.wait_ge(hi_made, 4 * j + k + 1)
                        act.wait_ge(lo_made, 4 * j + k + 1)
                    sign(j, k + 2, 1, 0)
                if conv:
                    scale_out(j, k, 2)
                if bring:
                    copy_in(j, k, 1)
                if stats:
                    sign(j, k + 2, 1, 1)
                if conv:
                    scale_out(j, k, 3)
                if bring:
                    copy_in(j, k, 2)
                    copy_in(j, k, 3)
                if stats:
                    sign(j, k + 2, 2, 0)

            act.wait_ge(w_var_ready, 1)
            act.activation(w_stat[:, 5:6], w_stat[:, 4:5], ACT.Sqrt).then_inc(w_root_ready, 1)
            for c in range(CHUNKS):
                copy_in(0, -3, c)
            act.wait_ge(w_bias_ready, M_FIL)
            for m in range(M_FIL):
                act.activation(filt[:, :, :, :, m], w_raw[:], ACT.Sign, bias=w_bias[:, m:m + 1]).then_inc(w_signed, 1)
                if m in (2, 3):
                    copy_in(0, -2, m - 2)
            act.wait_ge(consts_ready, 1)
            take_root(0, -2)
            act.wait_ge(thr_ready, 3)
            sign(0, 0, 1, 0)
            copy_in(0, -2, 2)
            sign(0, 0, 1, 1)
            copy_in(0, -2, 3)
            sign(0, 0, 2, 0)
            sign(0, 0, 2, 1)
            act.wait_ge(signed, 2)
            act.wait_ge(ratios_ready, 3)
            act.activation(hi_part[0][:], signs[0][:, 1].rearrange("p i a h -> p (i a h)"), ACT.Copy,
                           scale=ratio_hi[:, 0:1]).then_inc(hi_part1_made, 1)
            take_root(0, -1)
            sign(0, 0, 0, 0)
            sign(0, 0, 0, 1)
            for c in range(CHUNKS):
                copy_in(0, -1, c)
            act.wait_ge(thr_ready, 6)
            for n, a in ((1, 0), (1, 1), (2, 0)):
                sign(0, 1, n, a)
            act.wait_ge(y_scale_ready, 1)
            main_steps(act, step)

        @block.vector
        def _(dve):
            done = {"n": 0, "base": 0}

            def mark(ins):
                ins.then_inc(vec, 1)
                done["n"] += 1

            def count():
                return done["n"]

            def settle(n=None):
                dve.wait_ge(vec, done["base"] + (done["n"] if n is None else n))

            def link(ins):
                mark(ins)
                settle()

            tt, ts, stt = nc.vector.tensor_tensor, nc.vector.tensor_scalar, nc.vector.scalar_tensor_tensor

            nc.vector.memset(w_raw[0:C, :, 1, :], 0.0)
            nc.vector.memset(w_raw[3 * C:4 * C, :, 0, :], 0.0)
            for i in range(2):
                mark(nc.vector.memset(lane_stats[i][:], 1.0))
            nc.vector.memset(ones[:], 1.0)
            nc.vector.memset(eps_col[:], GN_EPS).then_inc(consts_ready, 1)

            def masks():
                dve.wait_ge(ident_ready, 1)
                mark(nc.vector.reduce_sum(own_group[:], ident[:].rearrange("p (g c) -> p g c", g=G), axis=AX.X))
                mark(nc.vector.reduce_sum(same_ch_row[:], ident[:].rearrange("p (g c) -> p c g", g=G), axis=AX.X))
                n = count()
                col = ident[0:GP, 0:GP].rearrange("p (c m) -> p m c", c=GC)
                mark(nc.vector.reduce_sum(own_filter[:], col[:, 0:M_FIL], axis=AX.X))
                mark(nc.vector.reduce_sum(same_col[:], col.rearrange("p m c -> p c m"), axis=AX.X))
                settle(n)
                nc.vector.tensor_copy(same_ch[:], same_ch_row[:].unsqueeze(1).broadcast_to([128, G, C]))\
                    .then_inc(same_ch_ready, 1)

            def filter_lanes():
                dve.wait_ge(w_loaded, 32)
                link(nc.vector.bn_stats(w_stat[0:96, 6:12], w_raw[0:96, :, 0, :]))
                link(nc.vector.bn_aggr(w_stat[0:96, 0:2], w_stat[0:96, 6:12]))
                link(tt(w_stat[0:96, 2:3], w_stat[0:96, 0:1], w_stat[0:96, 0:1], ALU.mult))
                tt(w_stat[0:96, 1:2], w_stat[0:96, 1:2], w_stat[0:96, 2:3], ALU.add).then_inc(w_lane_stats, 1)

            def filter_var():
                dve.wait_ge(w_summed, 1)
                link(ts(w_stat[:, 12:14], w_ps[:, 0:2], 1.0 / 96, None, ALU.mult))
                link(tt(w_stat[:, 3:4], w_stat[:, 12:13], w_stat[:, 12:13], ALU.mult))
                tt(w_stat[:, 4:5], w_stat[:, 13:14], w_stat[:, 3:4], ALU.subtract).then_inc(w_var_ready, 1)

            def filter_bias():
                dve.wait_ge(w_root_ready, 1)
                dve.wait_ge(w_var_ready, 1)
                link(nc.vector.reciprocal(w_stat[:, 14:15], w_stat[:, 5:6]))
                link(tt(w_stat[:, 14:15], w_stat[:, 14:15], w_stat[:, 4:5], ALU.mult))
                link(tt(w_stat[:, 15:16], w_stat[:, 14:15], w_stat[:, 5:6], ALU.add))
                for m in range(M_FIL):
                    u = -1.0 + m * 2.0 / (M_FIL - 1)
                    stt(w_bias[:, m:m + 1], w_stat[:, 15:16], 0.5 * u, w_stat[:, 12:13],
                        ALU.mult, ALU.subtract).then_inc(w_bias_ready, 1)

            def filter_gram():
                dve.wait_ge(gram_made, 1)
                link(tt(gram_prod[:], w_ps[0:GP, 0:GP].rearrange("p (c m) -> p m c", c=GC),
                        same_col[:].unsqueeze(1).broadcast_to([GP, M_FIL + 1, GC]), ALU.mult))
                link(nc.vector.reduce_sum(gram_lane[:], gram_prod[:], axis=AX.X))
                tt(gram_spread[:], own_filter[:].unsqueeze(2).broadcast_to([GP, M_FIL, M_FIL + 1]),
                   gram_lane[:].unsqueeze(1).broadcast_to([GP, M_FIL, M_FIL + 1]), ALU.mult).then_inc(gram_lanes, 1)

            def eliminate(m):
                r = M_FIL - 1 - m
                mark(nc.vector.reciprocal(inv[:, m:m + 1], gram[:, m, m:m + 1]))
                if r:
                    mark(tt(outer[:, m + 1:, m + 1:],
                            gram[:, m, m + 1:M_FIL].unsqueeze(2).broadcast_to([128, r, r + 1]),
                            gram[:, m, m + 1:].unsqueeze(1).broadcast_to([128, r, r + 1]), ALU.mult))
                settle()
                if r:
                    mark(stt(gram[:, m + 1:, m + 1:], outer[:, m + 1:, m + 1:], inv[:, m:m + 1],
                             gram[:, m + 1:, m + 1:], ALU.mult, ALU.subtract))
                n = count()
                mark(ts(neg_row[:, m, m + 1:], gram[:, m, m + 1:], inv[:, m:m + 1], -1.0, ALU.mult, ALU.mult))
                settle(n)

            neg_alpha = neg_row[:, :, M_FIL]

            def substitute():
                settle()
                for m in range(M_FIL - 1, 0, -1):
                    link(stt(neg_alpha[:, 0:m], neg_row[:, 0:m, m], neg_alpha[:, m:m + 1], neg_alpha[:, 0:m],
                             ALU.mult, ALU.add))

            def filter_parts():
                neg_w = w_eff[:].rearrange("p a o c -> p (a o c)")
                fl = [filt[:, :, :, :, m].rearrange("p a o c -> p (a o c)") for m in range(M_FIL)]
                dve.wait_ge(corners_zero, 2)
                mark(stt(w_stat[:, 6:11], neg_alpha, -1.0, neg_alpha, ALU.mult, ALU.max))
                link(ts(neg_w, fl[0], neg_alpha[:, 0:1], None, ALU.mult))
                mark(nc.vector.reduce_sum(size[:, 0:1], w_stat[:, 6:11], axis=AX.X))
                link(stt(neg_w, fl[1], neg_alpha[:, 1:2], neg_w, ALU.mult, ALU.add))
                mark(nc.vector.reciprocal(size[:, 1:2], size[:, 0:1]))
                ts(y_scale[:], size[:, 0:1], order[:, 0, 0:1], 1.0 / W_SCALE, ALU.mult, ALU.mult)\
                    .then_inc(y_scale_ready, 1)
                link(stt(neg_w, fl[2], neg_alpha[:, 2:3], neg_w, ALU.mult, ALU.add))
                mark(ts(size[:, 2:3], size[:, 1:2], -W_SCALE, None, ALU.mult))
                mark(nc.vector.reduce_sum(w_stat[:, 0:1], neg_alpha, axis=AX.X))
                link(stt(neg_w, fl[3], neg_alpha[:, 3:4], neg_w, ALU.mult, ALU.add))
                mark(stt(y_const[:], w_stat[:, 0:1], -1.0, w_stat[:, 1:2], ALU.mult, ALU.mult))
                link(stt(neg_w, fl[4], neg_alpha[:, 4:5], neg_w, ALU.mult, ALU.add))
                wm = [w_mm[:, i].rearrange("p a o c -> p (a o c)") for i in range(3)]
                ts(wm[0], neg_w, size[:, 2:3], None, ALU.mult).then_inc(w_ready, 1)
                dve.wait_ge(w_ready, 1)
                stt(wm[1], neg_w, size[:, 2:3], wm[0], ALU.mult, ALU.subtract).then_inc(w_ready, 1)
                ts(wm[2], wm[0], 1.0 / LO_SCALE, None, ALU.mult).then_inc(w_ready, 1)

            def sum_beta_bias():
                dve.wait_ge(bias_loaded, 16)
                dve.wait_ge(params_loaded, 32)
                link(tt(beta_bias[:], params[:, 0, :], params[:, 2, :], ALU.mult))
                mark(nc.vector.reduce_sum(w_stat[:, 1:2], beta_bias[:], axis=AX.X))

            def flat(b, n):
                return signs[b][:, n].rearrange("p i a h -> p (i a h)")

            def add_x(j, k, c):
                b, _ = place(j, k, 2)
                s, _ = place(j, k, UNROLL)
                dve.wait_ge(y_transposed, OPEN + CHUNKS * (4 * j + k) + c + 1)
                lo, hi = 16 * c, min(16 * (c + 1), W)
                stt(y_nat[b][:, C * lo:C * hi], y_ps[c % 2][0:ROWS, 0:C * (hi - lo)],
                    y_const[0:ROWS, :], x_nat[s][:, C * (1 + lo):C * (1 + hi)],
                    ALU.add, ALU.add).then_inc(y_added[c % 2], 1)

            def lane_moments(j, k, half, images=(0, 1)):
                b, _ = place(j, k, 2)
                for i in range(2):
                    dve.wait_ge(x_copied[i], 2 * (4 * j + k) + half + 1)
                for a in images:
                    mark(nc.vector.bn_stats(raw_stats[b][:, a, half, :],
                                            x_ch[b][:, a, 7 * half:7 * half + 7, :].rearrange("p i h -> p (i h)")))

            def spread_lanes(j, k):
                b, _ = place(j, k, 2)
                for a in range(2):
                    mark(nc.vector.bn_aggr(lane_stats[b][:, a, 1:3],
                                           raw_stats[b][:, a].rearrange("p i s -> p (i s)")))
                settle()
                tt(spread_stats[b][:], own_group[:].unsqueeze(2).broadcast_to([128, G, 6]),
                   lane_stats[b][:].rearrange("p a s -> p (a s)").unsqueeze(1).broadcast_to([128, G, 6]),
                   ALU.mult).then_inc(lanes_ready, 1)

            def pair_moments(j, k):
                q = 4 * j + k
                b, _ = place(j, k, 2)
                st = stat_ps[:, 0:G * 6].rearrange("p (g a s) -> p g a s", g=G, a=2)
                for a in range(2):
                    nc.vector.bn_aggr(moments[b][:, a, :], st[:, :, a, :]).then_inc(moments_ready, 1)

            def invert_root(j, k):
                dve.wait_ge(root_ready, 4 * j + k + 1)
                mark(nc.vector.reciprocal(inv_root[:], root[:]))
                return count()

            def divide_variance(j, k, n):
                b, _ = place(j, k, 2)
                dve.wait_ge(moments_ready, 2 * (4 * j + k + 1))
                settle(n)
                mark(stt(twice_dev[:], moments[b][:, :, 1], GN_EPS, inv_root[:], ALU.add, ALU.mult))
                return count()

            def add_root(n):
                settle(n)
                mark(tt(twice_dev[:], twice_dev[:], root[:], ALU.add))
                return count()

            def make_thresholds(j, k, n):
                b, _ = place(j, k, 2)
                settle(n)
                for n in range(N_ACT):
                    stt(neg_thr[b][:, n, :], twice_dev[:], order[:, 1, n:n + 1], moments[b][:, :, 0],
                        ALU.mult, ALU.subtract).then_inc(thr_ready, 1)

            def thresholds(j, k):
                make_thresholds(j, k, add_root(divide_variance(j, k, invert_root(j, k))))

            def weigh_sign(j, k, n):
                b, _ = place(j, k, 2)
                dve.wait_ge(signed, 6 * (4 * j + k) + 2 * n)
                mark(ts(hi_part[n - 1][:], flat(b, n), ratio_hi[:, n - 1:n], None, ALU.mult))

            def sum_high(j, k, i):
                b, _ = place(j, k, 2)
                ins = tt(window_rows(b, 0, REGIONS[i]), block_rows(half_hi, REGIONS[i]),
                         block_rows(flat(b, 0), REGIONS[i]), ALU.add)
                if i == len(REGIONS) - 1:
                    ins.then_inc(hi_made, 1)

            def step(j, k, load, bring, stats, weigh, conv):
                if weigh:
                    weigh_sign(j, k + 1, 1)
                    dve.wait_ge(signed, 6 * (4 * j + k + 1) + 4)
                if stats:
                    dve.wait_ge(gathered, 4 * j + k + 3)
                if weigh:
                    weigh_sign(j, k + 1, 2)
                    n = count()
                if stats:
                    pair_moments(j, k + 2)
                if weigh:
                    settle(n)
                    mark(tt(half_hi[:], hi_part[0][:], hi_part[1][:], ALU.add))
                    half = count()
                if stats:
                    n = invert_root(j, k + 2)
                if weigh:
                    settle(half)
                    dve.wait_ge(signed, 6 * (4 * j + k + 2))
                    dve.wait_ge(conv_done, OPEN + CHUNKS * (4 * j + k))
                    sum_high(j, k + 1, 0)
                if stats:
                    n = divide_variance(j, k + 2, n)
                if weigh:
                    sum_high(j, k + 1, 1)
                if stats:
                    n = add_root(n)
                if weigh:
                    sum_high(j, k + 1, 2)
                if stats:
                    make_thresholds(j, k + 2, n)
                if weigh:
                    sum_high(j, k + 1, 3)
                dve.wait_ge(y_stored[k % 2], 16 * (OPEN + 4 * j + 2 * (k // 2)))
                add_x(j, k, 0)
                add_x(j, k, 1)
                if bring:
                    lane_moments(j, k + AHEAD, 0)
                add_x(j, k, 2)
                if bring:
                    lane_moments(j, k + AHEAD, 1)
                    settle()
                    tt(dve_carrier[:], eps_col[:], eps_col[:], ALU.add)
                    spread_lanes(j, k + AHEAD)
                add_x(j, k, 3)

            filter_lanes()
            masks()
            filter_var()
            filter_bias()
            lane_moments(0, 0, 0)
            lane_moments(0, 0, 1)
            settle()
            spread_lanes(0, 0)
            lane_moments(0, 1, 0, images=(0,))
            dve.wait_ge(divisor_ready, 1)
            nc.vector.reciprocal(tmp[:, 5, 2:3], tmp[:, 5, 1:2]).then_inc(inverse_ready, 1)
            dve.wait_ge(gathered, 1)
            pair_moments(0, 0)
            dve.wait_ge(order_ready, 3)
            thresholds(0, 0)
            filter_gram()
            lane_moments(0, 1, 0, images=(1,))
            sum_beta_bias()
            dve.wait_ge(gram_summed, 1)
            link(nc.vector.tensor_copy(gram[:], w_ps[:, GRAM].rearrange("p (m n) -> p m n", m=M_FIL)))
            eliminate(0)
            eliminate(1)
            lane_moments(0, 1, 1)
            settle()
            spread_lanes(0, 1)
            eliminate(2)
            dve.wait_ge(gathered, 2)
            pair_moments(0, 1)
            eliminate(3)
            thresholds(0, 1)
            dve.wait_ge(ratios_ready, 3)
            weigh_sign(0, 0, 2)
            eliminate(4)
            dve.wait_ge(hi_part1_made, 1)
            link(tt(half_hi[:], hi_part[0][:], hi_part[1][:], ALU.add))
            dve.wait_ge(signed, 6)
            dve.wait_ge(pads_ready, 8)
            for i in range(len(REGIONS)):
                sum_high(0, 0, i)
            substitute()
            filter_parts()
            lane_moments(0, 2, 0)
            lane_moments(0, 2, 1)
            settle()
            spread_lanes(0, 2)

            start = done["n"]
            with dve.Fori(0, LOOP) as j:
                done["base"] = UNROLL * MARKS_PER_STEP * j
                for k in range(UNROLL):
                    step(j, k, **FULL)
                assert done["n"] - start == UNROLL * MARKS_PER_STEP, (done["n"] - start) / UNROLL
            done["base"], done["n"] = 0, start + UNROLL * MARKS_PER_STEP * LOOP
            for k in range(UNROLL):
                step(LOOP, k, **stages(UNROLL * LOOP + k))

        @block.tensor
        def _(pe):
            def bring_in(j, k, c):
                q = k + AHEAD
                s, uses = place(j, q, UNROLL)
                if c == 0:
                    pe.wait_ge(x_loaded[0][s], 32 * (uses + 1))
                if c == 2:
                    pe.wait_ge(x_loaded[1][s], 16 * (uses + 1))
                if not (isinstance(j, int) and 4 * j + q == 0 and c < 2):
                    pe.wait_ge(x_copied[c % 2], 2 * (4 * j + q) + c // 2)
                for i in range(CB[c]):
                    blk = 4 * c + i
                    last = nc.tensor.transpose(x_ps[c % 2][:, i * ROWS:(i + 1) * ROWS],
                                               x_nat[s][:, 128 * blk:128 * (blk + 1)], ident[0:ROWS, 0:ROWS])
                last.then_inc(x_transposed, 1)

            def gather_lanes(j, k):
                q = 4 * j + k + 2
                b, _ = place(j, k + 2, 2)
                pe.wait_ge(lanes_ready, q + 1)
                if not (isinstance(j, int) and q == 0):
                    pe.wait_ge(moments_ready, 2 * q)
                nc.tensor.matmul(stat_ps[:, 0:6 * G], same_ch[:].rearrange("p g c -> p (g c)"),
                                 spread_stats[b][:].rearrange("p g s -> p (g s)"),
                                 start=True, stop=True).then_inc(gathered, 1)

            PRODUCTS = [(0, 0), (0, 1), (1, 2)]

            def convolve(j, k, c, first_pair=False):
                b, uses = place(j, k, 2)
                bank = c % 2
                pe.wait_ge(y_scaled[bank], OPEN + 2 * (4 * j + k) + c // 2)
                even = s_even[b][:].rearrange("p s (r h) -> p s r h", h=HP)
                odd = s_odd[b][:].rearrange("p s (r h) -> p s r h", h=HP)
                for n, (part, kind) in enumerate(PRODUCTS):
                    if first_pair and c == 0:
                        pe.wait_ge(w_ready, n + 1)
                    if c == 0 and n in (0, 2):
                        made, shifted = ((hi_made, shifted_hi), (lo_made, shifted_lo))[part]
                        pe.wait_ge(made, 4 * j + k + 1)
                        pe.wait_ge(shifted[b], 32 * (uses + 1))
                    for t in range(TAPS):
                        first, end = n == 0 and t == 0, n == 2 and t == TAPS - 1
                        wt = w_mm[:, kind, t].rearrange("p o c -> p (o c)")
                        r0 = 2 * CB[0] * c
                        nc.tensor.matmul(conv_ps[bank][0:64, 0:CB[c] * ROWS], wt,
                                         even[:, part, r0:r0 + 2 * CB[c], t:t + H], start=first, stop=end)
                        last = nc.tensor.matmul(conv_ps[bank][64:128, 0:CB[c] * ROWS], wt,
                                                odd[:, part, r0:r0 + 2 * CB[c], t:t + H], start=first, stop=end)
                last.then_inc(conv_done, 1)

            def bring_out(j, k, c):
                bank = c % 2
                pe.wait_ge(y_scaled[bank], OPEN + 2 * (4 * j + k) + c // 2 + 1)
                pe.wait_ge(y_added[bank], OPEN + 2 * (4 * j + k) + c // 2)
                for i in range(CB[c]):
                    last = nc.tensor.transpose(y_ps[bank][0:ROWS, 128 * i:128 * (i + 1)],
                                               y_ch[bank][:, i * ROWS:(i + 1) * ROWS], ident[:])
                last.then_inc(y_transposed, 1)

            def step(j, k, load, bring, stats, weigh, conv, first_pair=False):
                if conv:
                    convolve(j, k, 0, first_pair=first_pair)
                    if stats:
                        gather_lanes(j, k)
                    convolve(j, k, 1)
                if bring:
                    bring_in(j, k, 0)
                if conv:
                    bring_out(j, k, 0)
                    convolve(j, k, 2)
                if bring:
                    bring_in(j, k, 1)
                if conv:
                    bring_out(j, k, 1)
                    convolve(j, k, 3)
                if bring:
                    bring_in(j, k, 2)
                if conv:
                    bring_out(j, k, 2)
                if bring:
                    bring_in(j, k, 3)
                if conv:
                    bring_out(j, k, 3)

            pe.wait_ge(w_lane_stats, 1)
            pe.wait_ge(consts_ready, 1)
            nc.tensor.matmul(w_ps[:, 0:2], ones[0:96, :], w_stat[0:96, 0:2], start=True, stop=True)\
                .then_inc(w_summed, 1)
            pe.wait_ge(ident_ready, 1)
            for c in range(CHUNKS):
                bring_in(0, -3, c)
            bring_in(0, -2, 0)
            bring_in(0, -2, 1)
            pe.wait_ge(same_ch_ready, 1)
            gather_lanes(0, -2)
            pe.wait_ge(w_signed, M_FIL)
            pe.wait_ge(w_copied, 1)
            for a in range(TAPS):
                for h in range(C // GC):
                    col = slice(GC * h, GC * (h + 1))
                    fc = filt[0:96, a, 0, col, :].rearrange("p c m -> p (c m)")
                    last = nc.tensor.matmul(w_ps[0:GP, 0:GP], fc, fc, start=a + h == 0,
                                            stop=(a + 1) * (h + 1) == TAPS * (C // GC))
            last.then_inc(gram_made, 1)
            bring_in(0, -2, 2)
            bring_in(0, -2, 3)
            pe.wait_ge(gram_lanes, 1)
            nc.tensor.matmul(w_ps[:, GRAM], ones[0:GP, :], gram_spread[:].rearrange("p m n -> p (m n)"),
                             start=True, stop=True).then_inc(gram_summed, 1)
            bring_in(0, -1, 0)
            bring_in(0, -1, 1)
            gather_lanes(0, -1)
            bring_in(0, -1, 2)
            bring_in(0, -1, 3)
            for _ in range(WARM):
                nc.tensor.matmul(y_ps[1][:, 0:128], ones[:], ones[:], start=True, stop=True)
            step(0, 0, **FULL, first_pair=True)
            with pe.Fori(0, LOOP) as j:
                for k in range(1, UNROLL + 1):
                    step(j, k, **FULL)
            for k in range(1, UNROLL):
                step(LOOP, k, **stages(UNROLL * LOOP + k))


MARKS_PER_STEP = 12


_INS = ["x", "L0_conv_W", "L0_conv_beta", "L0_conv_v", "L0_conv_bias"]


def kernel(**inputs):
    import numpy as np
    import concourse.bacc as bacc
    from concourse.bass_utils import run_bass_kernel_spmd

    nc = bacc.Bacc("TRN2", target_bir_lowering=False, num_devices=1)
    arrays, args = {}, []
    for name in _INS:
        a = np.ascontiguousarray(inputs[name])
        arrays[f"in_{name}"] = a
        args.append(nc.dram_tensor(f"in_{name}", a.shape, mybir.dt.from_np(a.dtype), kind="ExternalInput").ap())
    out = nc.dram_tensor("out_0", inputs["x"].shape, FP32, kind="ExternalOutput").ap()
    preact_conv_kernel(nc, *args, out)
    r = run_bass_kernel_spmd(nc, [arrays], core_ids=[0])
    return r.results[0]["out_0"]
```
